# Optimizing a Trainium2 kernel written in Bass

```python
import numpy as np
import jax
import jax.numpy as jnp

def _softmax(x, axis=-1):
    return jax.nn.softmax(x, axis=axis)

def _gelu(x):
    return jax.nn.gelu(x, approximate=True)

def _silu(x):
    return jax.nn.silu(x)

def _sigmoid(x):
    return jax.nn.sigmoid(x)

def _layernorm(x, axis=-1, eps=1e-05):
    m = jnp.mean(x, axis=axis, keepdims=True)
    v = jnp.var(x, axis=axis, keepdims=True)
    return (x - m) / jnp.sqrt(v + eps)

def _scatter_add(tgt, idx, src, axis=0):
    return tgt.at[idx].add(src)

def _segment_sum(src, seg, n):
    return jax.ops.segment_sum(src, seg, n)
kernel_name = 'mk_adaln_ffn_d2_seqx_r8_e472f6'

def setup_inputs(seed: int=0):
    np.random.seed(seed)
    _w = jnp.asarray

    def _rec_inputs():
        import jax
        import jax.numpy as jnp
        _rk = jax.random.key(seed)
        x = -0.0001538 + 1 * jax.random.normal(jax.random.fold_in(_rk, 1), (32, 128, 128), jnp.float32)
        _lenS = 128 - jax.random.randint(jax.random.fold_in(_rk, 7), (32,), 0, max(1, 128 // 4) + 1, jnp.int32)
        _lenS2 = 128 - jax.random.randint(jax.random.fold_in(_rk, 8), (32,), 0, max(1, 128 // 4) + 1, jnp.int32)
        cond_1024 = 0.00782532 + 1.00527 * jax.random.normal(jax.random.fold_in(_rk, 11), (32, 128), jnp.float32)
        return (x, cond_1024)
    x, cond_1024 = _rec_inputs()

    def _L0_cond_setup():
        import jax, jax.numpy as jnp
        import numpy as np
        NUM_EXPERTS = 4
        TOP_K = 2
        key = jax.random.key(seed)
        ks = jax.random.split(key, 16)
        B, L, D, E, H = (8, 96, 128, NUM_EXPERTS, 512)
        s = 0.02
        return {'context_c': jax.random.normal(ks[0], (B, L, D), jnp.float32), 'time_cond': jax.random.normal(ks[1], (B, D), jnp.float32), 'gate_w': jax.random.normal(ks[2], (3 * D, E), jnp.float32) * s, 'gate_b': jnp.zeros((E,), jnp.float32), 'time_w': jax.random.normal(ks[3], (D, 2 * E), jnp.float32) * s, 'time_b': jnp.zeros((2 * E,), jnp.float32), 'ew1': jax.random.normal(ks[4], (E, D, H), jnp.float32) * s, 'eb1': jnp.zeros((E, H), jnp.float32), 'ew2': jax.random.normal(ks[5], (E, H, D), jnp.float32) * s, 'eb2': jnp.zeros((E, D), jnp.float32), 'sw1': jax.random.normal(ks[6], (D, H), jnp.float32) * s, 'sb1': jnp.zeros((H,), jnp.float32), 'sw2': jax.random.normal(ks[7], (H, D), jnp.float32) * s, 'sb2': jnp.zeros((D,), jnp.float32)}
    _L0_cond_all = _L0_cond_setup()
    _L0_cond_in = {k: v for k, v in _L0_cond_all.items() if k in ('gate_w', 'gate_b', 'time_w', 'time_b', 'ew1', 'eb1', 'ew2', 'eb2', 'sw1', 'sb1', 'sw2', 'sb2')}
    del _L0_cond_all

    def _L0_ffn_setup():
        import jax, jax.numpy as jnp
        import numpy as np
        B, S, H = (2, 128, 128)
        E, F = (8, 512)
        GATE_TEMP = 0.1
        key = jax.random.key(seed)
        ks = jax.random.split(key, 6)
        s_h = 1.0 / np.sqrt(H)
        s_f = 1.0 / np.sqrt(F)
        return {'hidden_states': jax.random.normal(ks[0], (B, S, H), dtype=jnp.float32), 'w_router': jax.random.normal(ks[1], (H, E), dtype=jnp.float32) * s_h, 'w_gating': jax.random.normal(ks[2], (H, E), dtype=jnp.float32) * s_h, 'w_gate': jax.random.normal(ks[3], (E, H, F), dtype=jnp.float32) * s_h, 'w_up': jax.random.normal(ks[4], (E, H, F), dtype=jnp.float32) * s_h, 'w_down': jax.random.normal(ks[5], (E, F, H), dtype=jnp.float32) * s_f}
    _L0_ffn_all = _L0_ffn_setup()
    _L0_ffn_in = {k: v for k, v in _L0_ffn_all.items() if k in ('w_router', 'w_gating', 'w_gate', 'w_up', 'w_down')}
    del _L0_ffn_all

    def _L1_cond_setup():
        import jax, jax.numpy as jnp
        import numpy as np
        D_MODEL = 128
        D_FF = 512
        N_EXPERTS = 8
        TOP_K = 2
        N_SHARED = 2
        B, T = (4, 256)
        key = jax.random.key(seed)
        ks = jax.random.split(key, 9)
        Hs = D_FF // 2
        Hr = D_FF // 4
        inp = {'x': jax.random.normal(ks[0], (B, T, D_MODEL), dtype=jnp.float32), 't_emb': jax.random.normal(ks[1], (B, D_MODEL), dtype=jnp.float32), 'W_router': 0.01 * jax.random.normal(ks[2], (N_EXPERTS, 2 * D_MODEL), dtype=jnp.float32), 'router_bias': jnp.zeros((N_EXPERTS,), dtype=jnp.float32), 's_w1': 0.02 * jax.random.normal(ks[3], (N_SHARED, Hs, D_MODEL), dtype=jnp.float32), 's_w3': 0.02 * jax.random.normal(ks[4], (N_SHARED, Hs, D_MODEL), dtype=jnp.float32), 's_w2': 0.02 * jax.random.normal(ks[5], (N_SHARED, D_MODEL, Hs), dtype=jnp.float32), 'r_w1': 0.02 * jax.random.normal(ks[6], (N_EXPERTS, Hr, D_MODEL), dtype=jnp.float32), 'r_w2': 0.02 * jax.random.normal(ks[7], (N_EXPERTS, D_MODEL, Hr), dtype=jnp.float32)}
        return inp
    _L1_cond_all = _L1_cond_setup()
    _L1_cond_in = {k: v for k, v in _L1_cond_all.items() if k in ('W_router', 'router_bias', 's_w1', 's_w3', 's_w2', 'r_w1', 'r_w2')}
    del _L1_cond_all

    def _L1_ffn_setup():
        import jax, jax.numpy as jnp
        import numpy as np
        D_MODEL, D_FF, RANK = (128, 512, 32)
        B, S = (4, 512)
        key = jax.random.key(seed)
        ks = jax.random.split(key, 7)
        return {'x': jax.random.normal(ks[0], (B, S, D_MODEL), dtype=jnp.float32), 'U1': jax.random.normal(ks[1], (D_MODEL, RANK), dtype=jnp.float32) * 0.02, 'V1': jax.random.normal(ks[2], (RANK, D_FF), dtype=jnp.float32) * 0.02, 'b1': jnp.zeros((D_FF,), dtype=jnp.float32), 'U2': jax.random.normal(ks[3], (D_FF, RANK), dtype=jnp.float32) * 0.02, 'V2': jax.random.normal(ks[4], (RANK, D_MODEL), dtype=jnp.float32) * 0.02, 'b2': jnp.zeros((D_MODEL,), dtype=jnp.float32)}
    _L1_ffn_all = _L1_ffn_setup()
    _L1_ffn_in = {k: v for k, v in _L1_ffn_all.items() if k in ('U1', 'V1', 'b1', 'U2', 'V2', 'b2')}
    del _L1_ffn_all
    return {'x': x, 'cond_1024': cond_1024, 'L0_cond_gate_w': _L0_cond_in['gate_w'], 'L0_cond_gate_b': _L0_cond_in['gate_b'], 'L0_cond_time_w': _L0_cond_in['time_w'], 'L0_cond_time_b': _L0_cond_in['time_b'], 'L0_cond_ew1': _L0_cond_in['ew1'], 'L0_cond_eb1': _L0_cond_in['eb1'], 'L0_cond_ew2': _L0_cond_in['ew2'], 'L0_cond_eb2': _L0_cond_in['eb2'], 'L0_cond_sw1': _L0_cond_in['sw1'], 'L0_cond_sb1': _L0_cond_in['sb1'], 'L0_cond_sw2': _L0_cond_in['sw2'], 'L0_cond_sb2': _L0_cond_in['sb2'], 'L0_ffn_w_router': _L0_ffn_in['w_router'], 'L0_ffn_w_gating': _L0_ffn_in['w_gating'], 'L0_ffn_w_gate': _L0_ffn_in['w_gate'], 'L0_ffn_w_up': _L0_ffn_in['w_up'], 'L0_ffn_w_down': _L0_ffn_in['w_down'], 'L1_cond_W_router': _L1_cond_in['W_router'], 'L1_cond_router_bias': _L1_cond_in['router_bias'], 'L1_cond_s_w1': _L1_cond_in['s_w1'], 'L1_cond_s_w3': _L1_cond_in['s_w3'], 'L1_cond_s_w2': _L1_cond_in['s_w2'], 'L1_cond_r_w1': _L1_cond_in['r_w1'], 'L1_cond_r_w2': _L1_cond_in['r_w2'], 'L1_ffn_U1': _L1_ffn_in['U1'], 'L1_ffn_V1': _L1_ffn_in['V1'], 'L1_ffn_b1': _L1_ffn_in['b1'], 'L1_ffn_U2': _L1_ffn_in['U2'], 'L1_ffn_V2': _L1_ffn_in['V2'], 'L1_ffn_b2': _L1_ffn_in['b2']}

def reference(x, cond_1024, L0_cond_gate_w, L0_cond_gate_b, L0_cond_time_w, L0_cond_time_b, L0_cond_ew1, L0_cond_eb1, L0_cond_ew2, L0_cond_eb2, L0_cond_sw1, L0_cond_sb1, L0_cond_sw2, L0_cond_sb2, L0_ffn_w_router, L0_ffn_w_gating, L0_ffn_w_gate, L0_ffn_w_up, L0_ffn_w_down, L1_cond_W_router, L1_cond_router_bias, L1_cond_s_w1, L1_cond_s_w3, L1_cond_s_w2, L1_cond_r_w1, L1_cond_r_w2, L1_ffn_U1, L1_ffn_V1, L1_ffn_b1, L1_ffn_U2, L1_ffn_V2, L1_ffn_b2):
    import jax
    import jax.numpy as jnp

    def _L0_cond_ref(context_c, time_cond, gate_w, gate_b, time_w, time_b, ew1, eb1, ew2, eb2, sw1, sb1, sw2, sb2):
        import jax, jax.numpy as jnp
        import numpy as np
        NUM_EXPERTS = 4
        TOP_K = 2
        B, L, D = context_c.shape
        E, K = (NUM_EXPERTS, TOP_K)
        L_head = L_wrist = L // 3
        head = context_c[:, :L_head]
        wrist = context_c[:, L_head:L_head + L_wrist]
        proprio = context_c[:, L_head + L_wrist:]
        full_agg = context_c.mean(axis=1)
        hp_agg = jnp.concatenate([head, proprio], axis=1).mean(axis=1)
        wp_agg = jnp.concatenate([wrist, proprio], axis=1).mean(axis=1)
        gate_in = jnp.concatenate([full_agg, hp_agg, wp_agg], axis=-1)
        gate_logits = gate_in @ gate_w + gate_b
        mod = jax.nn.silu(time_cond) @ time_w + time_b
        scale, shift = jnp.split(mod, 2, axis=-1)
        gate_logits = gate_logits * (1.0 + scale) + shift
        gate_scores = jax.nn.softmax(gate_logits, axis=-1)
        topk_w, topk_i = jax.lax.top_k(gate_scores, K)
        topk_w = topk_w / (topk_w.sum(axis=-1, keepdims=True) + 1e-08)
        onehot = (topk_i[..., None] == jnp.arange(E)[None, None, :]).astype(context_c.dtype)
        w_be = jnp.sum(topk_w[..., None] * onehot, axis=1)
        mask = np.ones((E, L), dtype=np.float32)
        mask[1, L_head:L_head + L_wrist] = 0.0
        mask[2, :L_head] = 0.0
        mask = jnp.asarray(mask)
        out = jnp.zeros_like(context_c)
        for e in range(E):
            h = jax.nn.gelu(context_c @ ew1[e] + eb1[e], approximate=True)
            y = h @ ew2[e] + eb2[e]
            out = out + w_be[:, e][:, None, None] * mask[e][None, :, None] * y
        shared = jax.nn.gelu(context_c @ sw1 + sb1, approximate=True) @ sw2 + sb2
        return out + shared

    def _L0_ffn_ref(hidden_states, w_router, w_gating, w_gate, w_up, w_down):
        import jax, jax.numpy as jnp
        import numpy as np
        B, S, H = (2, 128, 128)
        E, F = (8, 512)
        GATE_TEMP = 0.1
        x = hidden_states
        router_probs = jax.nn.softmax(jnp.einsum('bsh,he->bse', x, w_router), axis=-1)
        gate_weights = jax.nn.softmax(jnp.einsum('bsh,he->bse', x, w_gating) / GATE_TEMP, axis=-1)
        g = jnp.einsum('bsh,ehf->ebsf', x, w_gate)
        u = jnp.einsum('bsh,ehf->ebsf', x, w_up)
        h = jax.nn.silu(g) * u
        expert_out = jnp.einsum('ebsf,efh->ebsh', h, w_down)
        cw = router_probs * gate_weights
        cw = cw / (jnp.sum(cw, axis=-1, keepdims=True) + 1e-09)
        out = jnp.einsum('ebsh,bse->bsh', expert_out, cw)
        return out

    def _L1_cond_ref(x, t_emb, W_router, router_bias, s_w1, s_w3, s_w2, r_w1, r_w2):
        import jax, jax.numpy as jnp
        import numpy as np
        D_MODEL = 128
        D_FF = 512
        N_EXPERTS = 8
        TOP_K = 2
        N_SHARED = 2
        B, T = (4, 256)
        Bn, Tn, C = x.shape
        N = Bn * Tn
        x_flat = x.reshape(N, C)
        t_flat = jnp.broadcast_to(t_emb[:, None, :], (Bn, Tn, C)).reshape(N, C)
        shared_out = jnp.zeros_like(x_flat)
        for e in range(N_SHARED):
            h = jax.nn.silu(x_flat @ s_w1[e].T) * (x_flat @ s_w3[e].T)
            shared_out = shared_out + h @ s_w2[e].T
        shared_out = shared_out / N_SHARED
        router_in = jnp.concatenate([x_flat, t_flat], axis=-1)
        s = jax.nn.sigmoid((router_in @ W_router.T).astype(jnp.float32))
        sel_scores = s + router_bias
        _, topk_idx = jax.lax.top_k(sel_scores, TOP_K)
        s_sel = jnp.take_along_axis(s, topk_idx, axis=1)
        denom = jnp.sum(s_sel, axis=1, keepdims=True)
        gates = jnp.where(denom > 1e-09, s_sel / (denom + 1e-09), 1.0 / TOP_K).astype(x.dtype)
        gates_full = jnp.sum(jax.nn.one_hot(topk_idx, N_EXPERTS, dtype=x.dtype) * gates[..., None], axis=1)
        routed_out = jnp.zeros_like(x_flat)
        for e in range(N_EXPERTS):
            h = jax.nn.gelu(x_flat @ r_w1[e].T, approximate=False)
            routed_out = routed_out + h @ r_w2[e].T * gates_full[:, e:e + 1]
        out = (shared_out + routed_out) / (N_SHARED + TOP_K)
        return out.reshape(Bn, Tn, C)

    def _L1_ffn_ref(x, U1, V1, b1, U2, V2, b2):
        import jax, jax.numpy as jnp
        import numpy as np
        D_MODEL, D_FF, RANK = (128, 512, 32)
        B, S = (4, 512)
        P = jnp.einsum('bsd,dr->bsr', x, U1)
        H = jax.nn.gelu(jnp.einsum('bsr,rf->bsf', P, V1) + b1)
        Q = jnp.einsum('bsf,fr->bsr', H, U2)
        return jnp.einsum('bsr,rd->bsd', Q, V2) + b2
    x = x + _L0_ffn_ref(_L0_cond_ref(x, cond_1024, L0_cond_gate_w, L0_cond_gate_b, L0_cond_time_w, L0_cond_time_b, L0_cond_ew1, L0_cond_eb1, L0_cond_ew2, L0_cond_eb2, L0_cond_sw1, L0_cond_sb1, L0_cond_sw2, L0_cond_sb2), L0_ffn_w_router, L0_ffn_w_gating, L0_ffn_w_gate, L0_ffn_w_up, L0_ffn_w_down)
    x = x + _L1_ffn_ref(_L1_cond_ref(x, cond_1024, L1_cond_W_router, L1_cond_router_bias, L1_cond_s_w1, L1_cond_s_w3, L1_cond_s_w2, L1_cond_r_w1, L1_cond_r_w2), L1_ffn_U1, L1_ffn_V1, L1_ffn_b1, L1_ffn_U2, L1_ffn_V2, L1_ffn_b2)
    return x

_drawn_inputs = setup_inputs


def setup_inputs(seed=0):
    import zlib

    import numpy as np

    out = dict(_drawn_inputs(seed))
    spreads = {'L0_cond_gate_b': (0.0, 0.1),
     'L0_cond_time_b': (0.0, 0.1),
     'L0_cond_eb1': (0.0, 0.1),
     'L0_cond_eb2': (0.0, 0.1),
     'L0_cond_sb1': (0.0, 0.1),
     'L0_cond_sb2': (0.0, 0.1),
     'L1_cond_router_bias': (0.0, 0.1),
     'L1_ffn_b1': (0.0, 0.1),
     'L1_ffn_b2': (0.0, 0.1)}
    factors = {}
    for name, (base, spread) in spreads.items():
        noise = np.random.default_rng([zlib.crc32(name.encode()), seed]).standard_normal(out[name].shape)
        drawn = base * np.exp(spread * noise) if base else spread * noise
        out[name] = jnp.asarray(drawn.astype(out[name].dtype))
    for name, factor in factors.items():
        out[name] = (out[name] * factor).astype(out[name].dtype)
    return out
```

```python
from contextlib import ExitStack

import concourse.bass as bass
from concourse import mybir

ALU = mybir.AluOpType
ACT = mybir.ActivationFunctionType
F32 = mybir.dt.float32
F32R = mybir.dt.float32r
AX = mybir.AxisListType.X

P = 128
NB = 32
NT = NB * P
BLK = 512
NBLK = NT // BLK
SEG = (0, 42, 86, 128)
LAG = 3
NH = LAG + 3
NS = 4
NZ = 4

SM = {}
_at = 0
for _name, _n in [("gw", 12), ("tw", 8), ("wrx", 8), ("wrt", 8), ("rw", 16), ("gb", 4), ("tb", 8), ("rb", 8),
                  ("eb1", 16), ("sb1", 4), ("eb2", 4), ("sb2", 1), ("b1", 4), ("b2", 1), ("cond", 32),
                  ("tri8", 64), ("tri4", 16), ("m1", 1), ("m2", 1), ("ident", 128), ("ones", 128)]:
    SM[_name] = (_at, _at + _n)
    _at += _n
SMALL = _at
AW = 1024
BW = 1536
CW = 3584
FW = 1280


class Engine:

    def __init__(self, sem):
        self.sem, self.n, self.queue, self.seen = sem, 0, [], {}

    def wait(self, *marks):
        for m in marks:
            if m is not None and self.seen.get(id(m[0]), 0) < m[1]:
                self.seen[id(m[0])] = m[1]
                self.queue.append(lambda e, m=m: e.wait_ge(m[0], m[1]))

    def do(self, fn):
        self.n += 1
        self.queue.append(lambda e: fn(e).then_inc(self.sem, 1))
        return self.sem, self.n

    def go(self, fn):
        self.queue.append(fn)

    def last(self):
        return self.sem, self.n

    def run(self, e):
        for fn in self.queue:
            fn(e)


class Flow:

    def __init__(self, sem):
        self.sem, self.n = sem, 0

    def dma(self, eng, out, in_):
        self.n += 16
        eng.go(lambda e: e.dma_start(out, in_).then_inc(self.sem, 16))
        return self.sem, self.n


class Banks:

    def __init__(self, banks):
        self.banks, self.k, self.freed = banks, 0, [None] * len(banks)

    def take(self):
        i = self.k % len(self.banks)
        self.k += 1
        return i, self.banks[i]


class Item:
    def __init__(self, kind, blk, ex, f, last):
        self.kind, self.blk, self.ex, self.f, self.last = kind, blk, ex, f, last
        self.lo, self.hi = 0, P
        if kind == "A" and ex == 2:
            self.hi = SEG[2]
        if kind == "A" and ex == 3:
            self.lo = SEG[1]
        self.w = self.hi - self.lo
        self.n = 4 * self.w


def plan():
    items = []
    for blk in range(NBLK):
        for ex in range(5):
            items += [Item("A", blk, ex, f, f == 3) for f in range(4)]
    for ex in range(8):
        for blk in range(NBLK):
            items += [Item("B", blk, ex, f, f == 3) for f in range(4)]
    for blk in range(NBLK):
        items += [Item("S", blk, f // 2, f % 2, False) for f in range(4)]
        items += [Item("R", blk, e, 0, e == 7) for e in range(8)]
        if blk:
            items += [Item("F", blk - 1, 0, f, f == 3) for f in range(4)]
    items += [Item("F", NBLK - 1, 0, f, f == 3) for f in range(4)]
    return items


def build(nc, x_d, small_d, wa_d, wb_d, wc_d, wf_d, scr_d, out_d):
    with ExitStack() as ctx:
        def sb(name, shape, dt=F32, c=None):
            return (c or ctx).enter_context(nc.sbuf_tensor(name, shape, dt))

        def flow(name):
            return Flow(ctx.enter_context(nc.semaphore(name)))

        pe, act, dve, pool, sp = [Engine(ctx.enter_context(nc.semaphore("s_" + n)))
                                  for n in ("pe", "act", "dve", "pool", "sp")]

        XT = sb("XT", [P, NBLK, BLK])
        XH = sb("XH", [P, NBLK, BLK], F32R)
        XL = sb("XL", [P, NBLK, BLK], F32R)
        sm = sb("sm", [P, SMALL])
        WBH = sb("WBH", [P, 2, BW], F32R)
        WBL = sb("WBL", [P, 2, BW], F32R)
        ST = sb("ST", [P, 2, BW])
        CWB = sb("CWB", [P, 2, 4 * BLK])
        Sg = sb("Sg", [P, NS, BLK])
        Hf = sb("Hf", [P, NS, BLK])
        HH = sb("HH", [P, NH, BLK], F32R)
        HL = sb("HL", [P, NH, BLK], F32R)
        TMP = sb("TMP", [P, 2, BLK])
        CB = sb("CB", [P, 2, BLK])
        LR = sb("LR", [P, NB, 16])
        TP = sb("TP", [P, NB, 8])
        WG = sb("WG", [P, NB, 4])
        Gs = sb("Gs", [P, 3, NB])
        Gm = sb("Gm", [P, 3, NB])
        sc = sb("sc", [P, NB])
        q0 = sb("q0", [P, 1024])
        q1 = sb("q1", [P, 1024])
        q2 = sb("q2", [P, 256])
        q3 = sb("q3", [P, 256])
        q4 = sb("q4", [P, 128])
        r0 = sb("r0", [P, 32])
        r1 = sb("r1", [P, 32])
        r2 = sb("r2", [P, 32])
        actx = ctx.enter_context(ExitStack())
        WAH = sb("WAH", [P, 5, AW], F32R, actx)
        WAL = sb("WAL", [P, 5, AW], F32R, actx)
        actx.close()
        WCH = sb("WCH", [P, CW], F32R)
        WCL = sb("WCL", [P, CW], F32R)
        U1H = sb("U1H", [P, P], F32R)
        U1L = sb("U1L", [P, P], F32R)
        V1H = sb("V1H", [P, BLK], F32R)
        V1S = sb("V1S", [P, BLK], F32R)
        U2S = sb("U2S", [P, 4, 4, 32], F32R)
        V2H = sb("V2H", [P, P], F32R)
        V2L = sb("V2L", [P, P], F32R)
        PH = sb("PH", [P, BLK], F32R)
        PS = sb("PS", [P, BLK], F32R)
        QS = sb("QS", [P, BLK], F32R)

        ps = [ctx.enter_context(nc.psum_tensor(f"ps{i}", [P, BLK], F32)) for i in range(8)]
        zb = Banks(ps[0:NZ])
        ob = Banks(ps[NZ:NZ + 2])
        ab = Banks(ps[NZ + 2:8])

        fx = [flow(f"f_x{i}") for i in range(NBLK)]
        fsm = flow("f_sm")
        fst = [flow("f_st0"), flow("f_st1")]
        fwa = [flow(f"f_wa{i}") for i in range(4)]
        fscr = [flow(f"f_scr{i}") for i in range(4)]
        fcb = [flow(f"f_cb{i}") for i in range(8)]
        fout = flow("f_out")

        def S(name):
            return sm[:, SM[name][0]:SM[name][1]]

        def col(name, i=0):
            a = SM[name][0] + i
            return sm[:, a:a + 1]

        def mm(ps_, w, x, start, stop):
            pe.go(lambda e: e.matmul(ps_, w, x, start=start, stop=stop))

        def mm_last(ps_, w, x, start, stop):
            return pe.do(lambda e: e.matmul(ps_, w, x, start=start, stop=stop))

        def matmuls(out, pairs, start=True, stop=True):
            for k, (w, x) in enumerate(pairs):
                f = mm_last if k == len(pairs) - 1 else mm
                mark = f(out, w, x, start and k == 0, stop and k == len(pairs) - 1)
            return mark

        def split(eng_hi, eng_lo, src, hi, lo, ready, free):
            eng_hi.wait(*ready, *free)
            if eng_hi is act:
                h = act.do(lambda e: e.activation(hi, src, ACT.Copy))
            else:
                h = eng_hi.do(lambda e: e.tensor_copy(hi, src))
            eng_lo.wait(h, *ready, *free)
            low = eng_lo.do(lambda e: e.tensor_tensor(lo, src, hi.bitcast(F32), ALU.subtract))
            return h, low

        m_sm = fsm.dma(sp, sm[:, :], small_d)
        m_x = [None] * NBLK
        m_x[0] = fx[0].dma(sp, XT[:, 0, :], x_d[:, 0:BLK])
        m_wa = [None] * 5
        stA = [ST[:, 0, 0:AW], ST[:, 1, 0:AW], Sg[:, 0:2, :].rearrange("p a n -> p (a n)"),
               Sg[:, 2:4, :].rearrange("p a n -> p (a n)")]
        for i in range(2):
            m_wa[i] = fst[i].dma(sp, stA[i], wa_d[:, i * AW:(i + 1) * AW])
        for b in range(1, NBLK):
            m_x[b] = fx[b].dma(sp, XT[:, b, :], x_d[:, b * BLK:(b + 1) * BLK])

        m_split_x = [None] * NBLK
        m_split_x[0] = split(dve, dve, XT[:, 0, :], XH[:, 0, :], XL[:, 0, :], [m_x[0]], [])
        m_wA = [[None, None] for _ in range(5)]
        for h in range(2):
            c = slice(h * 512, h * 512 + 512)
            m_wA[0][h] = split(act, dve, stA[0][:, c], WAH[:, 0, c], WAL[:, 0, c], [m_wa[0]], [])
        for h in range(2):
            c = slice(h * 512, h * 512 + 512)
            m_wA[1][h] = split(pool, pool, stA[1][:, c], WAH[:, 1, c], WAL[:, 1, c], [m_wa[1]], [])
        m_stage = [m_wA[0][1], m_wA[1][1]]

        def stage(slot, cols, src):
            sp.wait(*m_stage[slot])
            return fst[slot].dma(sp, ST[:, slot, 0:cols], src)

        def prep_a():
            for i in range(2, 5):
                m = stage(i % 2, AW, wa_d[:, i * AW:(i + 1) * AW])
                for h in range(2):
                    c = slice(h * 512, h * 512 + 512)
                    m_wA[i][h] = split(pool, pool, ST[:, i % 2, c], WAH[:, i, c], WAL[:, i, c], [m], [])
                m_stage[i % 2] = m_wA[i][1]

        for b in range(1, 2):
            m_split_x[b] = split(pool, pool, XT[:, b, :], XH[:, b, :], XL[:, b, :], [m_x[b]], [])
        prep_a()

        def prep_x():
            for b in range(2, NBLK):
                m_split_x[b] = split(pool, pool, XT[:, b, :], XH[:, b, :], XL[:, b, :], [m_x[b]], [])
                yield
                yield
                yield

        m_wB = {}
        m_wC = {}
        last_up = {}
        last_down = {}
        m_cw = {}
        m_out = []
        m_acc = [None, None]
        m_tmp = [None, None]
        m_xt = [None] * NBLK
        m_feat = [list(m_split_x[b]) if m_split_x[b] else None for b in range(NBLK)]
        cbf = [None, None]
        m_cwread = {}
        m_g = [None]
        m_scr = {}
        free_sg = [None] * NS
        free_hf = [[] for _ in range(NS)]
        free_h = [None] * NH
        k_tmp = [0]

        def dv(fn, *marks):
            dve.wait(*marks, dve.last())
            return dve.do(fn)

        def bc(ap, axis, shape):
            return ap.unsqueeze(axis).to_broadcast(shape)

        def gates():
            xv = XT[:, :, :].rearrange("p k n -> p (k n)").rearrange("p (b t) -> p b t", t=P)
            act.wait(m_sm)
            m_sc = act.do(lambda e: e.activation(sc[:, :], S("cond"), ACT.Silu))
            for k in range(3):
                dve.wait(*m_x, m_sm)
                dve.do(lambda e, k=k: e.tensor_reduce(Gs[:, k, :], xv[:, :, SEG[k]:SEG[k + 1]], AX, ALU.add))
                if k < 2:
                    yield
            h_, p_, w_ = Gs[:, 0, :], Gs[:, 1, :], Gs[:, 2, :]
            dv(lambda e: e.tensor_tensor(r0[:, :], h_, p_, ALU.add))
            dv(lambda e: e.tensor_tensor(r1[:, :], w_, p_, ALU.add))
            dv(lambda e: e.tensor_tensor(r2[:, :], r0[:, :], w_, ALU.add))
            dv(lambda e: e.tensor_scalar(Gm[:, 0, :], r2[:, :], 1.0 / 128, None, ALU.mult))
            dv(lambda e: e.tensor_scalar(Gm[:, 1, :], r0[:, :], 1.0 / 86, None, ALU.mult))
            dv(lambda e: e.tensor_scalar(Gm[:, 2, :], r1[:, :], 1.0 / 86, None, ALU.mult))
            yield
            gp = q0[:, 0:384].rearrange("p (k b e) -> p k b e", k=3, e=4)
            gw = S("gw").rearrange("p (k e) -> p k e", k=3)
            for k in range(3):
                m_gp = dv(lambda e, k=k: e.tensor_tensor(gp[:, k, :, :], bc(Gm[:, k, :], 2, [P, NB, 4]),
                                                         bc(gw[:, k, :], 1, [P, NB, 4]), ALU.mult))
            mp = q0[:, 384:640].rearrange("p (b e) -> p b e", e=8)
            m_mp = dv(lambda e: e.tensor_tensor(mp, bc(sc[:, :], 2, [P, NB, 8]), bc(S("tw"), 1, [P, NB, 8]),
                                                ALU.mult), m_sc)
            tp = q0[:, 640:896].rearrange("p (b e) -> p b e", e=8)
            m_tp = dv(lambda e: e.tensor_tensor(tp, bc(S("cond"), 2, [P, NB, 8]), bc(S("wrt"), 1, [P, NB, 8]),
                                                ALU.mult))
            yield
            i, bk = ab.take()
            pe.wait(m_mp, ab.freed[i])
            matmuls(bk[:, 0:128], [(S("ones"), q0[:, k * 128:k * 128 + 128]) for k in range(3)])
            m_gl = matmuls(bk[:, 128:384], [(S("ones"), q0[:, 384:640])])
            j, bj = ab.take()
            pe.wait(m_tp, ab.freed[j])
            m_t = matmuls(bj[:, 0:256], [(S("ones"), q0[:, 640:896])])
            yield
            v4 = lambda a: a.rearrange("p (b e) -> p b e", e=4)
            t = v4(q2[:, 0:128])
            s = v4(q2[:, 128:256])
            mod = q3[:, 0:256].rearrange("p (b e) -> p b e", e=8)
            dv(lambda e: e.tensor_tensor(t, v4(bk[:, 0:128]), bc(S("gb"), 1, [P, NB, 4]), ALU.add), m_gl)
            ab.freed[i] = dv(lambda e: e.tensor_tensor(mod, bk[:, 128:384].rearrange("p (b e) -> p b e", e=8),
                                                       bc(S("tb"), 1, [P, NB, 8]), ALU.add))
            ab.freed[j] = dv(lambda e: e.tensor_copy(TP[:, :, :], bj[:, 0:256].rearrange(
                "p (b e) -> p b e", e=8)), m_t)
            dv(lambda e: e.scalar_tensor_tensor(out=s, in0=mod[:, :, 0:4], scalar=1.0, in1=t, op0=ALU.add,
                                                op1=ALU.mult))
            dv(lambda e: e.tensor_tensor(t, s, mod[:, :, 4:8], ALU.add))
            dv(lambda e: e.tensor_reduce(r0[:, :], t, AX, ALU.max))
            m = dv(lambda e: e.tensor_tensor(s, t, bc(r0[:, :], 2, [P, NB, 4]), ALU.subtract))
            act.wait(m)
            m = act.do(lambda e: e.activation(t, s, ACT.Exp))
            yield
            dv(lambda e: e.tensor_reduce(r0[:, :], t, AX, ALU.add), m)
            dv(lambda e: e.reciprocal(r1[:, :], r0[:, :]))
            dv(lambda e: e.tensor_tensor(s, t, bc(r1[:, :], 2, [P, NB, 4]), ALU.mult))
            yield
            rank(s, S("tri4"), NB, 4, v4(q3[:, 0:128]))
            dv(lambda e: e.scalar_tensor_tensor(out=t, in0=v4(q3[:, 0:128]), scalar=1.5, in1=s, op0=ALU.is_lt,
                                                op1=ALU.mult))
            yield
            dv(lambda e: e.tensor_reduce(r0[:, :], t, AX, ALU.add))
            dv(lambda e: e.tensor_scalar(r1[:, :], r0[:, :], 1e-8, None, ALU.add))
            dv(lambda e: e.reciprocal(r2[:, :], r1[:, :]))
            m_g[0] = dv(lambda e: e.tensor_tensor(WG[:, :, :], t, bc(r2[:, :], 2, [P, NB, 4]), ALU.mult))

        def rank(s, tri, nt, ne, out):
            n = nt * ne * ne
            shape = [P, nt, ne, ne]
            v = lambda a: a[:, 0:n].rearrange("p (t e j) -> p t e j", e=ne, j=ne)
            tv = tri.rearrange("p (e j) -> p e j", e=ne)
            sj, se = bc(s, 2, shape), bc(s, 3, shape)
            dv(lambda e: e.tensor_tensor(v(q0), sj, se, ALU.is_equal))
            dv(lambda e: e.tensor_tensor(q1[:, 0:n].rearrange("p (t k) -> p t k", t=nt),
                                         q0[:, 0:n].rearrange("p (t k) -> p t k", t=nt),
                                         bc(tri, 1, [P, nt, ne * ne]), ALU.mult))
            dv(lambda e: e.tensor_tensor(v(q0), sj, se, ALU.is_gt))
            dv(lambda e: e.tensor_tensor(q0[:, 0:n], q0[:, 0:n], q1[:, 0:n], ALU.add))
            dv(lambda e: e.tensor_reduce(out, v(q0), AX, ALU.add))

        def spread(layer, g, m_w):
            i, bk = ab.take()
            pe.wait(m_w, ab.freed[i])
            m = pe.do(lambda e: e.transpose(bk[:, 0:P], q4[:, :], S("ident")))
            yield
            m = ab.freed[i] = dv(lambda e: e.tensor_copy(q3[:, 0:P], bk[:, 0:P]), m)
            sp.wait(m)
            m_scr[layer, g] = fscr[2 * layer + g].dma(sp, scr_d[layer, g], q3[:, 0:P])
            m_q3[0] = m_scr[layer, g]

        m_q3 = [None]

        def load_cw(g, ex):
            sp.wait(m_scr[0, g], *m_cwread.get(g, []))
            src = scr_d[0, g].rearrange("(e t) k -> e (t k)", e=8)[ex].partition_broadcast(P)
            m_cw[g, ex] = fcb[g].dma(sp, CWB[:, g, :], src)

        def load_gate(blk, ex):
            sp.wait(m_scr[1, blk // 4], *m_cwread.get(("r", ex), []))
            src = scr_d[1, blk // 4].rearrange("(e t) k -> e (t k)", e=8)[ex][
                (blk % 4) * BLK:(blk % 4) * BLK + BLK].partition_broadcast(P)
            m_cw["r", blk, ex] = fcb[ex].dma(sp, CWB[:, ex // 4, (ex % 4) * BLK:(ex % 4) * BLK + BLK], src)

        def route0(g):
            v = LR[:, 16 * g:16 * g + 16, :].rearrange("p t (c e) -> p t c e", c=2)
            s4 = [P, 16, 2, 8]
            u = q2[:, 0:256].rearrange("p (t c e) -> p t c e", c=2, e=8)
            w = q3[:, 0:256].rearrange("p (t c e) -> p t c e", c=2, e=8)
            ra, rb = r0[:, 0:32].rearrange("p (t c) -> p t c", c=2), r1[:, 0:32].rearrange("p (t c) -> p t c", c=2)
            dv(lambda e: e.tensor_reduce(ra, v, AX, ALU.max))
            m = dv(lambda e: e.tensor_tensor(u, v, bc(ra, 3, s4), ALU.subtract))
            act.wait(m, m_q3[0])
            dve.wait(m_q3[0])
            act.do(lambda e: e.activation(w[:, :, 0, :], u[:, :, 0, :], ACT.Exp))
            m = act.do(lambda e: e.activation(w[:, :, 1, :], u[:, :, 1, :], ACT.Exp, scale=10.0))
            yield
            dv(lambda e: e.tensor_reduce(ra, w, AX, ALU.add), m)
            dv(lambda e: e.reciprocal(rb, ra))
            dv(lambda e: e.tensor_tensor(u, w, bc(rb, 3, s4), ALU.mult))
            yield
            c = q3[:, 0:128].rearrange("p (t e) -> p t e", e=8)
            dv(lambda e: e.tensor_tensor(c, u[:, :, 0, :], u[:, :, 1, :], ALU.mult))
            dv(lambda e: e.tensor_reduce(r0[:, 0:16], c, AX, ALU.add))
            dv(lambda e: e.tensor_scalar(r1[:, 0:16], r0[:, 0:16], 1e-9, None, ALU.add))
            dv(lambda e: e.reciprocal(r2[:, 0:16], r1[:, 0:16]))
            m = dv(lambda e: e.tensor_tensor(q4[:, :].rearrange("p (e t) -> p t e", e=8), c,
                                             bc(r2[:, 0:16], 2, [P, 16, 8]), ALU.mult))
            yield
            yield from spread(0, g, m)
            load_cw(g, 0)

        def route1(g):
            v = LR[:, 16 * g:16 * g + 16, 0:8]
            s3 = [P, 16, 8]
            s = q2[:, 0:128].rearrange("p (t e) -> p t e", e=8)
            sel = q2[:, 128:256].rearrange("p (t e) -> p t e", e=8)
            rk = q3[:, 0:128].rearrange("p (t e) -> p t e", e=8)
            a = q3[:, 128:256].rearrange("p (t e) -> p t e", e=8)
            act.wait(dve.last())
            m = act.do(lambda e: e.activation(s, v, ACT.Sigmoid))
            yield
            dv(lambda e: e.tensor_tensor(sel, s, bc(S("rb"), 1, s3), ALU.add), m, m_q3[0])
            rank(sel, S("tri8"), 16, 8, rk)
            yield
            dv(lambda e: e.tensor_scalar(rk, rk, 1.5, None, ALU.is_lt))
            dv(lambda e: e.tensor_tensor(sel, rk, s, ALU.mult))
            dv(lambda e: e.tensor_reduce(r0[:, 0:16], sel, AX, ALU.add))
            dv(lambda e: e.tensor_scalar(r1[:, 0:16], r0[:, 0:16], 1e-9, None, ALU.add))
            dv(lambda e: e.reciprocal(r2[:, 0:16], r1[:, 0:16]))
            dv(lambda e: e.tensor_scalar(r0[:, 0:16], r0[:, 0:16], 1e-9, None, ALU.is_gt))
            yield
            dv(lambda e: e.tensor_tensor(r1[:, 0:16], r0[:, 0:16], r2[:, 0:16], ALU.mult))
            dv(lambda e: e.tensor_scalar(r2[:, 0:16], r0[:, 0:16], -0.5, 0.5, ALU.mult, ALU.add))
            dv(lambda e: e.tensor_tensor(a, s, bc(r1[:, 0:16], 2, s3), ALU.mult))
            dv(lambda e: e.tensor_tensor(s, a, bc(r2[:, 0:16], 2, s3), ALU.add))
            m = dv(lambda e: e.tensor_tensor(q4[:, :].rearrange("p (e t) -> p t e", e=8), s, rk, ALU.mult))
            yield
            yield from spread(1, g, m)

        def prep_b(ex):
            slot = ex % 2
            m = stage(slot, BW, wb_d[ex])
            m_wB[ex] = [None] * 3
            for k in range(3):
                yield
                c = slice(k * 512, k * 512 + 512)
                m_wB[ex][k] = split(pool, pool, ST[:, slot, c], WBH[:, slot, c], WBL[:, slot, c], [m],
                                    [last_down.get(("B", ex - 2))])
            m_stage[slot] = m_wB[ex][2]

        def prep_c():
            free = [last_down["A"]]
            for k in range(2):
                m = stage(k, 768, wc_d[:, k * 768:k * 768 + 768])
                pool.wait(m)
                m2 = pool.do(lambda e, k=k: e.tensor_scalar(ST[:, k, 512:768], ST[:, k, 512:768], 0.5, None,
                                                            ALU.mult))
                yield
                for c0, c1 in ((0, 512), (512, 768)):
                    mk = split(pool, pool, ST[:, k, c0:c1], WCH[:, k * 768 + c0:k * 768 + c1],
                               WCL[:, k * 768 + c0:k * 768 + c1], [m, m2], free)
                    yield
                m_stage[k] = mk
            for k in range(2):
                m = stage(k, 1024, wc_d[:, 1536 + k * 1024:2560 + k * 1024])
                for h in range(2):
                    a = 1536 + k * 1024 + h * 512
                    mk = split(pool, pool, ST[:, k, h * 512:h * 512 + 512], WCH[:, a:a + 512],
                               WCL[:, a:a + 512], [m], free)
                    yield
                m_stage[k] = mk
            m = stage(0, FW, wf_d)
            mk = split(pool, pool, ST[:, 0, 0:128], U1H[:, :], U1L[:, :], [m], free)
            yield
            pool.wait(m, *free)
            m1 = pool.do(lambda e: e.tensor_copy(V1H[:, :], ST[:, 0, 128:640]))
            dve.wait(m, m1, *free)
            m1 = dve.do(lambda e: e.scalar_tensor_tensor(
                out=V1S[:, :], in0=V1H[:, :].bitcast(F32), scalar=col("m2"), in1=ST[:, 0, 128:640], op0=ALU.mult,
                op1=ALU.add))
            yield
            u2 = ST[:, 0, 640:1152].rearrange("p (f r c) -> p f r c", f=4, r=4)
            pool.wait(m, *free)
            for r in (0, 2):
                mu = pool.do(lambda e, r=r: e.tensor_copy(U2S[:, :, r, :], u2[:, :, r, :]))
            pool.wait(mu)
            for r in (1, 3):
                mu = pool.do(lambda e, r=r: e.tensor_tensor(U2S[:, :, r, :], u2[:, :, r, :],
                                                            U2S[:, :, r - 1, :].bitcast(F32), ALU.subtract))
            yield
            mv = split(pool, pool, ST[:, 0, 1152:1280], V2H[:, :], V2L[:, :], [m], free)
            m_wC["all"] = [mv[1], m1]

        def xs(it):
            if it.w == P:
                return XH[:, it.blk, :], XL[:, it.blk, :]
            return [t[:, it.blk, :].rearrange("p (b t) -> p b t", t=P)[:, :, it.lo:it.hi] for t in (XH, XL)]

        def three(wh, wl, xh, xl):
            return [(wh, xh), (wh, xl), (wl, xh)]

        def first(it, out, wcols, ready):
            wh, wl = wcols
            i, bk = zb.take()
            pe.wait(*ready, zb.freed[i])
            o = bk[:, 0:it.n]
            if it.w != P:
                o = o.rearrange("p (b t) -> p b t", t=it.w)
            xh, xl = xs(it)
            out.append((i, bk, matmuls(o, three(wh, wl, xh, xl))))

        def up(it):
            it.z = []
            if it.kind == "A":
                a = it.f * P
                first(it, it.z, (WAH[:, it.ex, a:a + P], WAL[:, it.ex, a:a + P]),
                      [*m_wA[it.ex][0], *m_feat[it.blk]])
            elif it.kind == "B":
                for k in range(2):
                    a = k * 512 + it.f * P
                    s = it.ex % 2
                    first(it, it.z, (WBH[:, s, a:a + P], WBL[:, s, a:a + P]),
                          [*m_wB[it.ex][k], *m_feat[it.blk]])
            elif it.kind == "S":
                for k in range(2):
                    a = it.ex * 768 + k * 256 + it.f * P
                    first(it, it.z, (WCH[:, a:a + P], WCL[:, a:a + P]), [*m_wC["all"], *m_feat[it.blk]])
            elif it.kind == "R":
                a = 1536 + it.ex * 256
                first(it, it.z, (WCH[:, a:a + P], WCL[:, a:a + P]), m_feat[it.blk])
            else:
                i, bk = zb.take()
                pe.wait(m_p[0], zb.freed[i])
                it.z.append((i, bk, matmuls(bk[:, :], [(V1S[:, it.f * P:it.f * P + P], PS[:, :])])))
            if it.kind == "F":
                m_ps[0] = pe.last()
            else:
                last_up[it.blk] = pe.last()

        n_read = [0] * 8

        def middle(it, k):
            s, n = k % NS, it.n
            i, bk, m_z = it.z[0]
            f_hf = free_hf[s]
            if it.kind in ("A", "F"):
                fn = ACT.Gelu_apprx_tanh
                if it.kind == "F":
                    bias = col("b1", it.f)
                elif it.ex == 0:
                    bias = col("sb1", it.f)
                else:
                    bias = col("eb1", 4 * (it.ex - 1) + it.f)
                act.wait(m_z, m_sm, *f_hf)
                it.h = zb.freed[i] = act.do(lambda e: e.activation(Hf[:, s, 0:n], bk[:, 0:n], fn, bias=bias))
                return
            act.wait(m_z, free_sg[s])
            fn = ACT.Gelu if it.kind == "R" else ACT.Silu
            m = zb.freed[i] = act.do(lambda e: e.activation(Sg[:, s, :], bk[:, :], fn))
            if it.kind == "R":
                q = CWB[:, it.ex // 4, (it.ex % 4) * BLK:(it.ex % 4) * BLK + BLK]
                pool.wait(m, m_cw["r", it.blk, it.ex], *f_hf)
                it.h = pool.do(lambda e: e.tensor_tensor(Hf[:, s, :], Sg[:, s, :], q, ALU.mult))
                m_cwread["r", it.ex] = [it.h]
                n_read[it.ex] += 1
            else:
                j, bj, m_u = it.z[1]
                dve.wait(m, m_u, *f_hf)
                it.h = zb.freed[j] = dve.do(lambda e: e.tensor_tensor(Hf[:, s, :], bj[:, :], Sg[:, s, :], ALU.mult))
            free_sg[s] = it.h

        def parts(it, k):
            s, hs, n = k % NS, k % NH, it.n
            on_act = it.kind in ("B", "S", "F") or (it.kind == "A" and k % 2) or (it.kind == "R" and k % 2)
            it.parts = split(act if on_act else dve, dve, Hf[:, s, 0:n], HH[:, hs, 0:n], HL[:, hs, 0:n],
                             [it.h], [free_h[hs]])
            free_hf[s] = list(it.parts)

        unit = {}

        def down(it, k):
            hs, n = k % NH, it.n
            if it.kind == "A":
                a = 512 + it.f * P
                key, w, ready = "A", (WAH[:, it.ex, a:a + P], WAL[:, it.ex, a:a + P]), m_wA[it.ex][1]
            elif it.kind == "B":
                a = 1024 + it.f * P
                key, w, ready = "B", (WBH[:, it.ex % 2, a:a + P], WBL[:, it.ex % 2, a:a + P]), m_wB[it.ex][2]
            elif it.kind == "F":
                key, w, ready = "F", None, []
            else:
                a = it.ex * 768 + 512 + it.f * P if it.kind == "S" else 1536 + it.ex * 256 + P
                key, w, ready = "C", (WCH[:, a:a + P], WCL[:, a:a + P]), []
            new = key not in unit
            if new:
                r = ab if key == "F" else ob
                unit[key] = (r,) + r.take()
                pe.wait(unit[key][0].freed[unit[key][1]])
            r, i, bk = unit[key]
            pe.wait(*it.parts, *ready)
            if key == "F":
                u = U2S[:, it.f, :, :].rearrange("p r c -> p (r c)")
                pairs = [(u, HH[:, hs, :]), (u, HL[:, hs, :])]
            else:
                pairs = three(*w, HH[:, hs, 0:n], HL[:, hs, 0:n])
            m = free_h[hs] = matmuls(bk[:, 0:n], pairs, start=new, stop=it.last)
            if it.kind == "A":
                last_down["A"] = m
            if it.kind == "B":
                last_down["B", it.ex] = m
            if it.last:
                del unit[key]
                it.o = (r, i, bk, m)
                return True

        def finish(it):
            r, i, bk, m = it.o
            c = it.blk % 2
            t = k_tmp[0] % 2
            n, w = it.n, it.w
            if it.kind == "A":
                if it.ex == 0:
                    dve.wait(m, m_sm, *(cbf[c] or []))
                    m_acc[c] = r.freed[i] = dve.do(lambda e: e.tensor_scalar(CB[:, c, :], bk[:, :], col("sb2"), None,
                                                                             ALU.add))
                    return
                ex = it.ex - 1
                k_tmp[0] += 1
                dve.wait(m, m_g[0], m_tmp[t])
                wg = WG[:, 4 * it.blk:4 * it.blk + 4, ex:ex + 1].to_broadcast([P, 4, w])
                v = lambda a: a[:, 0:n].rearrange("p (b t) -> p b t", t=w)
                md = r.freed[i] = dve.do(lambda e: e.scalar_tensor_tensor(
                    out=v(TMP[:, t, :]), in0=v(bk), scalar=col("eb2", ex), in1=wg, op0=ALU.add, op1=ALU.mult))
                acc = CB[:, c, :].rearrange("p (b t) -> p b t", t=P)[:, :, it.lo:it.hi]
                pool.wait(md, m_acc[c])
                m_acc[c] = m_tmp[t] = pool.do(lambda e: e.tensor_tensor(acc, acc, v(TMP[:, t, :]), ALU.add))
                if it.ex == 4:
                    gens.append(close_a(it.blk))
            elif it.kind == "B":
                k_tmp[0] += 1
                g = it.blk // 4
                q = CWB[:, g, (it.blk % 4) * BLK:(it.blk % 4) * BLK + BLK]
                dve.wait(m, m_cw[g, it.ex], m_tmp[t])
                md = r.freed[i] = dve.do(lambda e: e.tensor_tensor(TMP[:, t, :], bk[:, :], q, ALU.mult))
                m_cwread[g] = [md]
                if it.blk % 4 == 3:
                    if it.ex < 7:
                        load_cw(g, it.ex + 1)
                    else:
                        for e in range(4 * g, 4 * g + 4):
                            m_cwread["r", e] = [md]
                xt = XT[:, it.blk, :]
                pool.wait(md, m_xt[it.blk])
                m_tmp[t] = m_xt[it.blk] = pool.do(lambda e: e.tensor_tensor(xt, xt, TMP[:, t, :], ALU.add))
                if it.ex == 7:
                    gens.append(close_b(it.blk))
            elif it.kind == "R":
                gens.append(close_c(it))
            else:
                gens.append(close_f(it))

        def close_a(blk):
            c = blk % 2
            m = m_acc[c]
            parts_ = split(act, dve, CB[:, c, :], XH[:, blk, :], XL[:, blk, :], [m], [last_up[blk]])
            m_feat[blk] = list(parts_)
            yield
            i, bk = ab.take()
            pe.wait(m, m_sm, ab.freed[i])
            for t in range(4):
                mk = matmuls(bk[:, t * 16:t * 16 + 16], [(CB[:, c, t * P:t * P + P], S("rw"))])
            cbf[c] = [*parts_, mk]
            yield
            dve.wait(mk)
            ab.freed[i] = dve.do(lambda e: e.tensor_copy(LR[:, 4 * blk:4 * blk + 4, :],
                                                         bk[:, 0:64].rearrange("p (t e) -> p t e", e=16)))
            if blk % 4 == 3:
                yield
                yield from route0(blk // 4)

        def close_b(blk):
            parts_ = split(act, dve, XT[:, blk, :], XH[:, blk, :], XL[:, blk, :], [m_xt[blk]], [last_up[blk]])
            m_feat[blk] = list(parts_)
            yield
            i, bk = ab.take()
            pe.wait(m_xt[blk], ab.freed[i])
            for t in range(4):
                mk = matmuls(bk[:, t * 8:t * 8 + 8], [(XT[:, blk, t * P:t * P + P], S("wrx"))])
            yield
            dve.wait(mk)
            ab.freed[i] = dve.do(lambda e: e.tensor_tensor(
                LR[:, 4 * blk:4 * blk + 4, 0:8], bk[:, 0:32].rearrange("p (t e) -> p t e", e=8),
                TP[:, 4 * blk:4 * blk + 4, :], ALU.add))
            if blk % 4 == 3:
                yield
                yield from route1(blk // 4)

        next_gate = [0] * 8

        def load_gates():
            for e, b in enumerate(next_gate):
                if b < NBLK and (1, b // 4) in m_scr and ("r", e) in m_cwread and n_read[e] == b:
                    load_gate(b, e)
                    next_gate[e] += 1

        m_p = [None]
        m_ph = [None]
        m_ps = [None]
        m_qs = [None]

        def close_c(it):
            r, i, bk, m = it.o
            blk = it.blk
            t = k_tmp[0] % 2
            k_tmp[0] += 1
            act.wait(m, m_tmp[t])
            mt = r.freed[i] = act.do(lambda e: e.activation(TMP[:, t, :], bk[:, :], ACT.Copy, scale=0.25))
            parts_ = split(dve, dve, TMP[:, t, :], XH[:, blk, :], XL[:, blk, :], [mt], [last_up[blk]])
            m_tmp[t] = parts_[1]
            yield
            i, bk = zb.take()
            pe.wait(*parts_, *m_wC["all"], zb.freed[i])
            m = matmuls(bk[:, :], three(U1H[:, :], U1L[:, :], XH[:, blk, :], XL[:, blk, :]))
            last_up[blk] = m
            act.wait(m, m_ph[0])
            mh = act.do(lambda e: e.activation(PH[:, :], bk[:, :], ACT.Copy))
            dve.wait(mh, m, m_ps[0])
            m_p[0] = zb.freed[i] = dve.do(lambda e: e.scalar_tensor_tensor(
                out=PS[:, :], in0=PH[:, :].bitcast(F32), scalar=col("m1"), in1=bk[:, :], op0=ALU.mult, op1=ALU.add))
            m_ph[0] = m_p[0]

        def close_f(it):
            r, i, bk, m = it.o
            blk = it.blk
            act.wait(m, m_ph[0])
            mh = act.do(lambda e: e.activation(PH[:, :], bk[:, :], ACT.Copy))
            dve.wait(mh, m, m_qs[0])
            mq = r.freed[i] = m_ph[0] = dve.do(lambda e: e.scalar_tensor_tensor(
                out=QS[:, :], in0=PH[:, :].bitcast(F32), scalar=col("m2"), in1=bk[:, :], op0=ALU.mult, op1=ALU.add))
            yield
            j, bj = zb.take()
            pe.wait(mq, zb.freed[j])
            m = matmuls(bj[:, :], [(V2H[:, :], QS[:, :]), (V2L[:, :], QS[:, :])])
            m_qs[0] = m
            yield
            c = blk % 2
            dve.wait(m, *(cbf[c] or []))
            my = zb.freed[j] = dve.do(lambda e: e.scalar_tensor_tensor(
                out=CB[:, c, :], in0=bj[:, :], scalar=col("b2"), in1=XT[:, blk, :], op0=ALU.add, op1=ALU.add))
            sp.wait(my)
            cbf[c] = [fout_b[blk].dma(sp, out_d[:, blk * BLK:blk * BLK + BLK], CB[:, c, :])]
            m_out.append(cbf[c][0])

        fout_b = [flow(f"f_o{i}") for i in range(NBLK)]

        items = plan()
        first_slot = {}
        for k, it in enumerate(items):
            first_slot.setdefault((it.kind, it.ex), k)
            first_slot.setdefault(("blk", it.kind, it.blk), k)
        gens = []
        starts = {0: [gates(), prep_x()], first_slot["blk", "A", 5]: [prep_b(0)],
                  first_slot["B", 0] + LAG + 2: [prep_c()]}
        for ex in range(1, 8):
            starts.setdefault(first_slot["B", ex - 1] + (LAG + 3 if ex > 1 else LAG + 2 + 14), []).append(prep_b(ex))

        n = len(items)
        for k in range(n + LAG + 12):
            load_gates()
            gens += starts.get(k, [])
            live = []
            for g in gens[:]:
                try:
                    next(g)
                    live.append(g)
                except StopIteration:
                    pass
            gens[:] = live
            for b in range(NBLK):
                if m_feat[b] is None and m_split_x[b]:
                    m_feat[b] = list(m_split_x[b])
            if k < n:
                up(items[k])
                middle(items[k], k)
            if 1 <= k <= n:
                parts(items[k - 1], k - 1)
            if LAG <= k < n + LAG:
                it = items[k - LAG]
                if down(it, k - LAG):
                    finish(it)
        assert not gens and len(m_out) == NBLK
        sp.wait(*m_out, *m_scr.values())

        block = ctx.enter_context(nc.Block())

        @block.sync
        def _(e):
            sp.run(e)

        @block.tensor
        def _(e):
            pe.run(e)

        @block.scalar
        def _(e):
            act.run(e)

        @block.vector
        def _(e):
            dve.run(e)

        @block.gpsimd
        def _(e):
            pool.run(e)


def kernel(**inputs):
    import numpy as np
    import concourse.bacc as bacc
    from concourse.bass_utils import run_bass_kernel_spmd

    a = {k: np.asarray(v) for k, v in inputs.items()}
    f32 = np.float32
    perm = np.r_[0:42, 84:128, 42:84]

    def rows(w):
        return w.reshape(-1, P, w.shape[-1]).transpose(1, 0, 2).reshape(P, -1)

    def cols(v):
        return v.reshape(-1, P).T

    def every(v):
        return np.broadcast_to(v.reshape(1, -1), (P, v.size))

    x = a["x"][:, perm, :].reshape(NT, P).T
    part = np.arange(P)[:, None] // 32
    wr = a["L1_cond_W_router"]
    small = {
        "gw": rows(a["L0_cond_gate_w"]), "tw": a["L0_cond_time_w"], "wrx": wr[:, :P].T, "wrt": wr[:, P:].T,
        "rw": np.concatenate([a["L0_ffn_w_router"], a["L0_ffn_w_gating"]], 1),
        "gb": every(a["L0_cond_gate_b"]), "tb": every(a["L0_cond_time_b"]), "rb": every(a["L1_cond_router_bias"]),
        "eb1": cols(a["L0_cond_eb1"]), "sb1": cols(a["L0_cond_sb1"]), "eb2": cols(a["L0_cond_eb2"]),
        "sb2": cols(a["L0_cond_sb2"]), "b1": cols(a["L1_ffn_b1"]), "b2": cols(a["L1_ffn_b2"]),
        "cond": a["cond_1024"].T,
        "tri8": every(np.tril(np.ones((8, 8), f32), -1)), "tri4": every(np.tril(np.ones((4, 4), f32), -1)),
        "m1": -(part % 2).astype(f32), "m2": -(part // 2).astype(f32),
        "ident": np.eye(P, dtype=f32), "ones": np.ones((P, P), f32),
    }
    small = np.concatenate([small[n] for n in SM], 1)
    wa = [a["L0_cond_sw1"], rows(a["L0_cond_sw2"])]
    for e in range(4):
        wa += [a["L0_cond_ew1"][e], rows(a["L0_cond_ew2"][e])]
    wb = np.stack([np.concatenate([a["L0_ffn_w_gate"][e], a["L0_ffn_w_up"][e], rows(a["L0_ffn_w_down"][e])], 1)
                   for e in range(8)])
    wc = []
    for e in range(2):
        wc += [a["L1_cond_s_w1"][e].T, a["L1_cond_s_w3"][e].T, rows(a["L1_cond_s_w2"][e].T)]
    for e in range(8):
        wc += [a["L1_cond_r_w1"][e].T, a["L1_cond_r_w2"][e].T]
    u2 = rows(np.tile(a["L1_ffn_U2"], (1, 4)))
    wf = [np.tile(a["L1_ffn_U1"], (1, 4)), np.tile(a["L1_ffn_V1"], (4, 1)), u2, np.tile(a["L1_ffn_V2"], (4, 1))]

    nc = bacc.Bacc("TRN2", target_bir_lowering=False, num_devices=1)
    arrays, args = {}, []
    for name, v in [("x", x), ("small", small), ("wa", np.concatenate(wa, 1)), ("wb", wb),
                    ("wc", np.concatenate(wc, 1)), ("wf", np.concatenate(wf, 1))]:
        v = np.ascontiguousarray(v)
        arrays[f"in_{name}_dram"] = v
        args.append(nc.dram_tensor(f"in_{name}_dram", v.shape, mybir.dt.from_np(v.dtype), kind="ExternalInput").ap())
    args.append(nc.dram_tensor("scratch", (2, 2, P, P), F32, kind="Internal").ap())
    args.append(nc.dram_tensor("out_0_dram", (P, NT), F32, kind="ExternalOutput").ap())
    build(nc, *args)
    r = run_bass_kernel_spmd(nc, [arrays], core_ids=[0])
    y = r.results[0]["out_0_dram"].T.reshape(NB, P, P)
    back = np.argsort(perm)
    return np.ascontiguousarray(y[:, back, :])
```

```python
from contextlib import ExitStack

import concourse.bass as bass
from concourse import mybir

ALU = mybir.AluOpType
ACT = mybir.ActivationFunctionType
F32 = mybir.dt.float32
F32R = mybir.dt.float32r
AX = mybir.AxisListType.X

P = 128
NB = 32
NT = NB * P
BLK = 512
NBLK = NT // BLK
SEG = (0, 42, 86, 128)
LAG = 5
NH = LAG + 1
NS = 4
NG = 3
NZ = 4
WARM = 2

SM = {}
_at = 0
for _name, _n in [("gw", 12), ("tw", 8), ("wrx", 8), ("wrt", 8), ("rw", 16), ("gb", 4), ("tb", 8), ("rb", 8),
                  ("eb1", 16), ("sb1", 4), ("eb2", 4), ("sb2", 1), ("b1", 4), ("b2", 1), ("cond", 32),
                  ("tri8", 64), ("tri4", 16), ("m1", 1), ("m2", 1), ("ident", 128), ("ones", 128)]:
    SM[_name] = (_at, _at + _n)
    _at += _n
SMALL = _at
AW = 1024
BW = 1536
CW = 3584
FW = 1280


class Engine:

    def __init__(self, sem):
        self.sem, self.n, self.queue, self.seen = sem, 0, [], {}

    def wait(self, *marks):
        for m in marks:
            if m is not None and self.seen.get(id(m[0]), 0) < m[1]:
                self.seen[id(m[0])] = m[1]
                self.queue.append(lambda e, m=m: e.wait_ge(m[0], m[1]))

    def do(self, fn):
        self.n += 1
        self.queue.append(lambda e: fn(e).then_inc(self.sem, 1))
        return self.sem, self.n

    def go(self, fn):
        self.queue.append(fn)

    def last(self):
        return self.sem, self.n

    def run(self, e):
        for fn in self.queue:
            fn(e)


class Flow:

    def __init__(self, sem):
        self.sem, self.n = sem, 0

    def dma(self, eng, out, in_):
        self.n += 16
        eng.go(lambda e: e.dma_start(out, in_).then_inc(self.sem, 16))
        return self.sem, self.n


class Banks:

    def __init__(self, banks):
        self.banks, self.k, self.freed = banks, 0, [None] * len(banks)

    def take(self):
        i = self.k % len(self.banks)
        self.k += 1
        return i, self.banks[i]


class Item:

    def __init__(self, kind, blk, ex, f, last):
        self.kind, self.blk, self.ex, self.f, self.last = kind, blk, ex, f, last
        self.lo, self.hi = 0, P
        if kind == "A" and ex == 2:
            self.hi = SEG[2]
        if kind == "A" and ex == 3:
            self.lo = SEG[1]
        self.w = self.hi - self.lo
        self.n = 4 * self.w


def pause(n):
    for _ in range(n):
        yield


def plan():
    items = []
    for pair in range(0, NBLK, 2):
        for blk in (pair, pair + 1):
            items += [Item("A", blk, 0, f, f == 3) for f in range(4)]
        for blk in (pair, pair + 1):
            for ex in range(1, 5):
                items += [Item("A", blk, ex, f, f == 3) for f in range(4)]
    for ex in range(8):
        for blk in range(NBLK):
            items += [Item("B", blk, ex, f, f == 3) for f in range(4)]

    def shared(blk):
        return [Item("S", blk, f // 2, f % 2, False) for f in range(4)]

    def routed(blk):
        return [Item("R", blk, e, 0, e == 7) for e in range(8)]

    def final(blk):
        return [Item("F", blk, 0, f, f == 3) for f in range(4)]

    for b in range(0, NBLK, 2):
        items += shared(b)
        if b:
            items += final(b - 2)
        items += shared(b + 1)
        if b and b + 2 < NBLK:
            items += final(b - 1)
        items += routed(b) + routed(b + 1)
    items += final(NBLK - 3) + [None] + final(NBLK - 2) + [None] * 4 + final(NBLK - 1)
    return items


def build(nc, x_d, small_d, wa_d, wb_d, wc_d, wf_d, scr_d, out_d):
    with ExitStack() as ctx:
        def sb(name, shape, dt=F32, c=None):
            return (c or ctx).enter_context(nc.sbuf_tensor(name, shape, dt))

        def flow(name):
            return Flow(ctx.enter_context(nc.semaphore(name)))

        pe, act, dve, pool, sp = [Engine(ctx.enter_context(nc.semaphore("s_" + n)))
                                  for n in ("pe", "act", "dve", "pool", "sp")]

        XT = sb("XT", [P, NBLK, BLK])
        XH = sb("XH", [P, NBLK, BLK], F32R)
        XL = sb("XL", [P, NBLK, BLK], F32R)
        sm = sb("sm", [P, SMALL])
        WBH = sb("WBH", [P, 2, BW], F32R)
        WBL = sb("WBL", [P, 2, BW], F32R)
        ST = sb("ST", [P, 2, BW])
        CWB = sb("CWB", [P, 2, 4 * BLK])
        Sg = sb("Sg", [P, NG, BLK])
        Hf = sb("Hf", [P, NS, BLK])
        HH = sb("HH", [P, NH, BLK], F32R)
        HL = sb("HL", [P, NH, BLK], F32R)
        TMP = sb("TMP", [P, 2, BLK])
        CB = sb("CB", [P, 2, BLK])
        LR = sb("LR", [P, NB, 16])
        TP = sb("TP", [P, NB, 8])
        WG = sb("WG", [P, NB, 4])
        Gs = sb("Gs", [P, 3, NB])
        Gm = sb("Gm", [P, 3, NB])
        sc = sb("sc", [P, NB])
        q0 = sb("q0", [P, 1024])
        q1 = sb("q1", [P, 1024])
        q2 = sb("q2", [P, 256])
        q3 = sb("q3", [P, 256])
        q4 = sb("q4", [P, 128])
        r0 = sb("r0", [P, 32])
        r1 = sb("r1", [P, 32])
        r2 = sb("r2", [P, 32])
        actx = ctx.enter_context(ExitStack())
        WAH = sb("WAH", [P, 5, AW], F32R, actx)
        WAL = sb("WAL", [P, 5, AW], F32R, actx)
        actx.close()
        WCH = sb("WCH", [P, CW], F32R)
        WCL = sb("WCL", [P, CW], F32R)
        U1H = sb("U1H", [P, P], F32R)
        U1L = sb("U1L", [P, P], F32R)
        V1H = sb("V1H", [P, BLK], F32R)
        V1S = sb("V1S", [P, BLK], F32R)
        U2S = sb("U2S", [P, 4, 4, 32], F32R)
        V2H = sb("V2H", [P, P], F32R)
        V2L = sb("V2L", [P, P], F32R)
        PH = sb("PH", [P, BLK], F32R)
        PS = sb("PS", [P, 2, BLK], F32R)
        QS = sb("QS", [P, BLK], F32R)

        ps = [ctx.enter_context(nc.psum_tensor(f"ps{i}", [P, BLK], F32)) for i in range(8)]
        zb = Banks(ps[0:NZ])
        ob = Banks(ps[NZ:NZ + 2])
        ab = Banks(ps[NZ + 2:8])

        fx = [flow(f"f_x{i}") for i in range(NBLK)]
        fsm = flow("f_sm")
        fst = [flow("f_st0"), flow("f_st1")]
        fwa = [flow(f"f_wa{i}") for i in range(6)]
        fscr = [flow(f"f_scr{i}") for i in range(4)]
        fcb = [flow(f"f_cb{i}") for i in range(8)]
        fout = flow("f_out")

        def S(name):
            return sm[:, SM[name][0]:SM[name][1]]

        def col(name, i=0):
            a = SM[name][0] + i
            return sm[:, a:a + 1]

        def mm(ps_, w, x, start, stop):
            pe.go(lambda e: e.matmul(ps_, w, x, start=start, stop=stop))

        def mm_last(ps_, w, x, start, stop):
            return pe.do(lambda e: e.matmul(ps_, w, x, start=start, stop=stop))

        def matmuls(out, pairs, start=True, stop=True):
            for k, (w, x, *marks) in enumerate(pairs):
                pe.wait(*marks)
                f = mm_last if k == len(pairs) - 1 else mm
                mark = f(out, w, x, start and k == 0, stop and k == len(pairs) - 1)
            return mark

        def split(eng_hi, eng_lo, src, hi, lo, ready, free):
            eng_hi.wait(*ready, *free)
            if eng_hi is act:
                h = act.do(lambda e: e.activation(hi, src, ACT.Copy))
            else:
                h = eng_hi.do(lambda e: e.tensor_copy(hi, src))
            eng_lo.wait(h, *ready, *free)
            low = eng_lo.do(lambda e: e.tensor_tensor(lo, src, hi.bitcast(F32), ALU.subtract))
            return h, low

        m_x = [None] * NBLK
        m_x[0] = fx[0].dma(sp, XT[:, 0, :], x_d[:, 0:BLK])
        stage_a = [ST[:, 0, 0:AW], ST[:, 1, 0:AW], CWB[:, 0, 0:AW], CWB[:, 0, AW:2 * AW], CWB[:, 1, 0:AW]]
        m_wa0 = [fwa[0].dma(sp, stage_a[0][:, 0:512], wa_d[:, 0:512])]
        m_sm = fsm.dma(sp, sm[:, :], small_d)
        m_wa0.append(fwa[1].dma(sp, stage_a[0][:, 512:AW], wa_d[:, 512:AW]))
        m_x[1] = fx[1].dma(sp, XT[:, 1, :], x_d[:, BLK:2 * BLK])
        for b in range(2, NBLK):
            m_x[b] = fx[b].dma(sp, XT[:, b, :], x_d[:, b * BLK:(b + 1) * BLK])
        m_wa = [None, fst[1].dma(sp, stage_a[1], wa_d[:, AW:2 * AW])]
        for i in range(2, 5):
            m_wa.append(fwa[i].dma(sp, stage_a[i], wa_d[:, i * AW:(i + 1) * AW]))

        m_split_x = [None] * NBLK
        m = pool.do(lambda e: e.memset(Hf[:, 0, :], 0.0))
        pe.wait(m)
        m_warm = matmuls(ps[NZ - 1][:, :], [(Hf[:, 0, 0:P], Hf[:, 0, :])] * WARM)
        m_split_x[0] = split(dve, dve, XT[:, 0, :], XH[:, 0, :], XL[:, 0, :], [m_x[0]], [])
        m_wA = [[None, None] for _ in range(5)]
        for h in range(2):
            c = slice(h * 512, h * 512 + 512)
            m_wA[0][h] = split(act, dve if h == 0 else pool, stage_a[0][:, c], WAH[:, 0, c], WAL[:, 0, c],
                               [m_wa0[h]], [])
        act.wait(m_sm)
        m_sc = act.do(lambda e: e.activation(sc[:, :], S("cond"), ACT.Silu))
        m_split_x[1] = split(dve, pool, XT[:, 1, :], XH[:, 1, :], XL[:, 1, :], [m_x[1]], [])
        m_stage = [m_wA[0][0] + m_wA[0][1], None]

        def prep_a():
            for i in range(1, 5):
                for h in range(2):
                    c = slice(h * 512, h * 512 + 512)
                    m_wA[i][h] = split(act, pool, stage_a[i][:, c], WAH[:, i, c], WAL[:, i, c], [m_wa[i]], [])
                    yield from pause(2)
            m_stage[1] = m_wA[1][0] + m_wA[1][1]
            for g, r in ((0, (2, 3)), (1, (4,))):
                m_cwread[g] = [m for i in r for mm_ in m_wA[i] for m in mm_]

        def stage(slot, cols, src):
            assert m_stage[slot]
            sp.wait(*m_stage[slot])
            m_stage[slot] = None
            return fst[slot].dma(sp, ST[:, slot, 0:cols], src)

        def prep_x():
            for b in range(2, NBLK):
                m_split_x[b] = split(dve, pool, XT[:, b, :], XH[:, b, :], XL[:, b, :], [m_x[b]], [])
                yield from pause(4)

        m_wB = {}
        m_wC = {}
        last_up = {}
        last_down = {}
        m_cw = {}
        m_out = []
        m_acc = [None, None]
        m_tmp = [None, None]
        m_xt = [None] * NBLK
        m_feat = [list(m_split_x[b]) if m_split_x[b] else None for b in range(NBLK)]
        cbf = [None, None]
        m_cwread = {}
        m_g = [None]
        m_scr = {}
        free_sg = [None] * NG
        free_hf = [[m_warm]] + [[] for _ in range(NS - 1)]
        free_h = [None] * NH
        k_tmp = [0]

        def dv(fn, *marks):
            dve.wait(*marks, dve.last())
            return dve.do(fn)

        def bc(ap, axis, shape):
            return ap.unsqueeze(axis).to_broadcast(shape)

        def gates():
            xv = XT[:, :, :].rearrange("p k n -> p (k n)").rearrange("p (b t) -> p b t", t=P)
            for k in range(3):
                dve.wait(*m_x, m_sm)
                dve.do(lambda e, k=k: e.tensor_reduce(Gs[:, k, :], xv[:, :, SEG[k]:SEG[k + 1]], AX, ALU.add))
                if k < 2:
                    yield
            h_, p_, w_ = Gs[:, 0, :], Gs[:, 1, :], Gs[:, 2, :]
            dv(lambda e: e.tensor_tensor(r0[:, :], h_, p_, ALU.add))
            dv(lambda e: e.tensor_tensor(r1[:, :], w_, p_, ALU.add))
            dv(lambda e: e.tensor_tensor(r2[:, :], r0[:, :], w_, ALU.add))
            dv(lambda e: e.tensor_scalar(Gm[:, 0, :], r2[:, :], 1.0 / 128, None, ALU.mult))
            dv(lambda e: e.tensor_scalar(Gm[:, 1, :], r0[:, :], 1.0 / 86, None, ALU.mult))
            dv(lambda e: e.tensor_scalar(Gm[:, 2, :], r1[:, :], 1.0 / 86, None, ALU.mult))
            yield
            gp = q0[:, 0:384].rearrange("p (k b e) -> p k b e", k=3, e=4)
            gw = S("gw").rearrange("p (k e) -> p k e", k=3)
            for k in range(3):
                m_gp = dv(lambda e, k=k: e.tensor_tensor(gp[:, k, :, :], bc(Gm[:, k, :], 2, [P, NB, 4]),
                                                         bc(gw[:, k, :], 1, [P, NB, 4]), ALU.mult))
            mp = q0[:, 384:640].rearrange("p (b e) -> p b e", e=8)
            m_mp = dv(lambda e: e.tensor_tensor(mp, bc(sc[:, :], 2, [P, NB, 8]), bc(S("tw"), 1, [P, NB, 8]),
                                                ALU.mult), m_sc)
            tp = q0[:, 640:896].rearrange("p (b e) -> p b e", e=8)
            m_tp = dv(lambda e: e.tensor_tensor(tp, bc(S("cond"), 2, [P, NB, 8]), bc(S("wrt"), 1, [P, NB, 8]),
                                                ALU.mult))
            yield from pause(5)
            i, bk = ab.take()
            pe.wait(m_mp, ab.freed[i])
            matmuls(bk[:, 0:128], [(S("ones"), q0[:, k * 128:k * 128 + 128]) for k in range(3)])
            m_gl = matmuls(bk[:, 128:384], [(S("ones"), q0[:, 384:640])])
            j, bj = ab.take()
            pe.wait(m_tp, ab.freed[j])
            m_t = matmuls(bj[:, 0:256], [(S("ones"), q0[:, 640:896])])
            yield
            v4 = lambda a: a.rearrange("p (b e) -> p b e", e=4)
            t = v4(q2[:, 0:128])
            s = v4(q2[:, 128:256])
            mod = q3[:, 0:256].rearrange("p (b e) -> p b e", e=8)
            dv(lambda e: e.tensor_tensor(t, v4(bk[:, 0:128]), bc(S("gb"), 1, [P, NB, 4]), ALU.add), m_gl)
            ab.freed[i] = dv(lambda e: e.tensor_tensor(mod, bk[:, 128:384].rearrange("p (b e) -> p b e", e=8),
                                                       bc(S("tb"), 1, [P, NB, 8]), ALU.add))
            ab.freed[j] = dv(lambda e: e.tensor_copy(TP[:, :, :], bj[:, 0:256].rearrange(
                "p (b e) -> p b e", e=8)), m_t)
            dv(lambda e: e.scalar_tensor_tensor(out=s, in0=mod[:, :, 0:4], scalar=1.0, in1=t, op0=ALU.add,
                                                op1=ALU.mult))
            dv(lambda e: e.tensor_tensor(t, s, mod[:, :, 4:8], ALU.add))
            dv(lambda e: e.tensor_reduce(r0[:, :], t, AX, ALU.max))
            m = dv(lambda e: e.tensor_tensor(s, t, bc(r0[:, :], 2, [P, NB, 4]), ALU.subtract))
            act.wait(m)
            m = act.do(lambda e: e.activation(t, s, ACT.Exp))
            yield
            dv(lambda e: e.tensor_reduce(r0[:, :], t, AX, ALU.add), m)
            dv(lambda e: e.reciprocal(r1[:, :], r0[:, :]))
            dv(lambda e: e.tensor_tensor(s, t, bc(r1[:, :], 2, [P, NB, 4]), ALU.mult))
            yield
            for k, _ in enumerate(rank(s, S("tri4"), NB, 4, v4(q3[:, 0:128]))):
                if k % 2:
                    yield
            dv(lambda e: e.scalar_tensor_tensor(out=t, in0=v4(q3[:, 0:128]), scalar=1.5, in1=s, op0=ALU.is_lt,
                                                op1=ALU.mult))
            yield
            dv(lambda e: e.tensor_reduce(r0[:, :], t, AX, ALU.add))
            dv(lambda e: e.tensor_scalar(r1[:, :], r0[:, :], 1e-8, None, ALU.add))
            dv(lambda e: e.reciprocal(r2[:, :], r1[:, :]))
            m_g[0] = dv(lambda e: e.tensor_tensor(WG[:, :, :], t, bc(r2[:, :], 2, [P, NB, 4]), ALU.mult))

        def rank(s, tri, nt, ne, out):
            n = nt * ne * ne
            shape = [P, nt, ne, ne]
            v = lambda a: a[:, 0:n].rearrange("p (t e j) -> p t e j", e=ne, j=ne)
            sj, se = bc(s, 2, shape), bc(s, 3, shape)
            dv(lambda e: e.tensor_tensor(v(q0), sj, se, ALU.is_equal))
            yield
            dv(lambda e: e.tensor_tensor(q1[:, 0:n].rearrange("p (t k) -> p t k", t=nt),
                                         q0[:, 0:n].rearrange("p (t k) -> p t k", t=nt),
                                         bc(tri, 1, [P, nt, ne * ne]), ALU.mult))
            yield
            dv(lambda e: e.tensor_tensor(v(q0), sj, se, ALU.is_gt))
            yield
            dv(lambda e: e.tensor_tensor(q0[:, 0:n], q0[:, 0:n], q1[:, 0:n], ALU.add))
            yield
            dv(lambda e: e.tensor_reduce(out, v(q0), AX, ALU.add))

        def spread(layer, g, m_w):
            yield from pause(3)
            i, bk = ab.take()
            pe.wait(m_w, ab.freed[i])
            m = pe.do(lambda e: e.transpose(bk[:, 0:P], q4[:, :], S("ident")))
            yield
            m = ab.freed[i] = dv(lambda e: e.tensor_copy(q3[:, 0:P], bk[:, 0:P]), m)
            sp.wait(m)
            m_scr[layer, g] = fscr[2 * layer + g].dma(sp, scr_d[layer, g], q3[:, 0:P])
            m_q3[0] = m_scr[layer, g]

        m_q3 = [None]

        def load_cw(g, ex):
            sp.wait(m_scr[0, g], *m_cwread.get(g, []))
            src = scr_d[0, g].rearrange("(e t) k -> e (t k)", e=8)[ex].partition_broadcast(P)
            m_cw[g, ex] = fcb[g].dma(sp, CWB[:, g, :], src)

        def load_gate(blk, ex):
            sp.wait(m_scr[1, blk // 4], *m_cwread.get(("r", ex), []))
            src = scr_d[1, blk // 4].rearrange("(e t) k -> e (t k)", e=8)[ex][
                (blk % 4) * BLK:(blk % 4) * BLK + BLK].partition_broadcast(P)
            m_cw["r", blk, ex] = fcb[ex].dma(sp, CWB[:, ex // 4, (ex % 4) * BLK:(ex % 4) * BLK + BLK], src)

        def route0(g):
            v = LR[:, 16 * g:16 * g + 16, :].rearrange("p t (c e) -> p t c e", c=2)
            s4 = [P, 16, 2, 8]
            u = q2[:, 0:256].rearrange("p (t c e) -> p t c e", c=2, e=8)
            w = q3[:, 0:256].rearrange("p (t c e) -> p t c e", c=2, e=8)
            ra, rb = r0[:, 0:32].rearrange("p (t c) -> p t c", c=2), r1[:, 0:32].rearrange("p (t c) -> p t c", c=2)
            dv(lambda e: e.tensor_reduce(ra, v, AX, ALU.max))
            m = dv(lambda e: e.tensor_tensor(u, v, bc(ra, 3, s4), ALU.subtract))
            act.wait(m, m_q3[0])
            dve.wait(m_q3[0])
            act.do(lambda e: e.activation(w[:, :, 0, :], u[:, :, 0, :], ACT.Exp))
            m = act.do(lambda e: e.activation(w[:, :, 1, :], u[:, :, 1, :], ACT.Exp, scale=10.0))
            yield from pause(2)
            dv(lambda e: e.tensor_reduce(ra, w, AX, ALU.add), m)
            dv(lambda e: e.reciprocal(rb, ra))
            yield
            dv(lambda e: e.tensor_tensor(u, w, bc(rb, 3, s4), ALU.mult))
            yield
            c = q3[:, 0:128].rearrange("p (t e) -> p t e", e=8)
            dv(lambda e: e.tensor_tensor(c, u[:, :, 0, :], u[:, :, 1, :], ALU.mult))
            dv(lambda e: e.tensor_reduce(r0[:, 0:16], c, AX, ALU.add))
            yield
            dv(lambda e: e.tensor_scalar(r1[:, 0:16], r0[:, 0:16], 1e-9, None, ALU.add))
            dv(lambda e: e.reciprocal(r2[:, 0:16], r1[:, 0:16]))
            m = dv(lambda e: e.tensor_tensor(q4[:, :].rearrange("p (e t) -> p t e", e=8), c,
                                             bc(r2[:, 0:16], 2, [P, 16, 8]), ALU.mult))
            yield
            yield from spread(0, g, m)
            load_cw(g, 0)

        def route1(g):
            v = LR[:, 16 * g:16 * g + 16, 0:8]
            s3 = [P, 16, 8]
            s = q2[:, 0:128].rearrange("p (t e) -> p t e", e=8)
            sel = q2[:, 128:256].rearrange("p (t e) -> p t e", e=8)
            rk = q3[:, 0:128].rearrange("p (t e) -> p t e", e=8)
            a = q3[:, 128:256].rearrange("p (t e) -> p t e", e=8)
            act.wait(dve.last())
            m = act.do(lambda e: e.activation(s, v, ACT.Sigmoid))
            yield from pause(2)
            dv(lambda e: e.tensor_tensor(sel, s, bc(S("rb"), 1, s3), ALU.add), m, m_q3[0])
            yield from rank(sel, S("tri8"), 16, 8, rk)
            yield
            dv(lambda e: e.tensor_scalar(rk, rk, 1.5, None, ALU.is_lt))
            dv(lambda e: e.tensor_tensor(sel, rk, s, ALU.mult))
            dv(lambda e: e.tensor_reduce(r0[:, 0:16], sel, AX, ALU.add))
            dv(lambda e: e.tensor_scalar(r1[:, 0:16], r0[:, 0:16], 1e-9, None, ALU.add))
            yield
            dv(lambda e: e.reciprocal(r2[:, 0:16], r1[:, 0:16]))
            dv(lambda e: e.tensor_scalar(r0[:, 0:16], r0[:, 0:16], 1e-9, None, ALU.is_gt))
            yield
            dv(lambda e: e.tensor_tensor(r1[:, 0:16], r0[:, 0:16], r2[:, 0:16], ALU.mult))
            dv(lambda e: e.tensor_scalar(r2[:, 0:16], r0[:, 0:16], -0.5, 0.5, ALU.mult, ALU.add))
            dv(lambda e: e.tensor_tensor(a, s, bc(r1[:, 0:16], 2, s3), ALU.mult))
            dv(lambda e: e.tensor_tensor(s, a, bc(r2[:, 0:16], 2, s3), ALU.add))
            m = dv(lambda e: e.tensor_tensor(q4[:, :].rearrange("p (e t) -> p t e", e=8), s, rk, ALU.mult))
            yield
            yield from spread(1, g, m)

        def prep_b(ex):
            slot = ex % 2
            m = stage(slot, BW, wb_d[ex])
            yield from pause(6)
            m_wB[ex] = [None] * 3
            for k in range(3):
                yield
                c = slice(k * 512, k * 512 + 512)
                m_wB[ex][k] = split(dve, pool, ST[:, slot, c], WBH[:, slot, c], WBL[:, slot, c], [m],
                                    [last_down.get(("B", ex - 2))])
            m_stage[slot] = m_wB[ex][2]

        def prep_c():
            free = [last_down["A"]]
            for k in range(2):
                m = stage(k, 768, wc_d[:, k * 768:k * 768 + 768])
                pool.wait(m)
                m2 = pool.do(lambda e, k=k: e.tensor_scalar(ST[:, k, 512:768], ST[:, k, 512:768], 0.5, None,
                                                            ALU.mult))
                yield
                for c0, c1 in ((0, 512), (512, 768)):
                    mk = split(dve, pool, ST[:, k, c0:c1], WCH[:, k * 768 + c0:k * 768 + c1],
                               WCL[:, k * 768 + c0:k * 768 + c1], [m, m2], free)
                    yield
                m_stage[k] = mk
            for k in range(2):
                m = stage(k, 1024, wc_d[:, 1536 + k * 1024:2560 + k * 1024])
                for h in range(2):
                    a = 1536 + k * 1024 + h * 512
                    mk = split(dve, pool, ST[:, k, h * 512:h * 512 + 512], WCH[:, a:a + 512],
                               WCL[:, a:a + 512], [m], free)
                    yield
                m_stage[k] = mk
            m = stage(0, FW, wf_d)
            mk = split(dve, pool, ST[:, 0, 0:128], U1H[:, :], U1L[:, :], [m], free)
            yield
            dve.wait(m, *free)
            m1 = dve.do(lambda e: e.tensor_copy(V1H[:, :], ST[:, 0, 128:640]))
            dve.wait(m, m1, *free)
            m1 = dve.do(lambda e: e.scalar_tensor_tensor(
                out=V1S[:, :], in0=V1H[:, :].bitcast(F32), scalar=col("m2"), in1=ST[:, 0, 128:640], op0=ALU.mult,
                op1=ALU.add))
            yield
            u2 = ST[:, 0, 640:1152].rearrange("p (f r c) -> p f r c", f=4, r=4)
            pool.wait(m, *free)
            for r in (0, 2):
                mu = pool.do(lambda e, r=r: e.tensor_copy(U2S[:, :, r, :], u2[:, :, r, :]))
            pool.wait(mu)
            for r in (1, 3):
                mu = pool.do(lambda e, r=r: e.tensor_tensor(U2S[:, :, r, :], u2[:, :, r, :],
                                                            U2S[:, :, r - 1, :].bitcast(F32), ALU.subtract))
            yield
            mv = split(dve, pool, ST[:, 0, 1152:1280], V2H[:, :], V2L[:, :], [m], free)
            m_stage[0] = [m1, mu, *mv]
            m_wC["all"] = [m1, mv[1]]

        def xs(it):
            if it.w == P:
                return XH[:, it.blk, :], XL[:, it.blk, :]
            return [t[:, it.blk, :].rearrange("p (b t) -> p b t", t=P)[:, :, it.lo:it.hi] for t in (XH, XL)]

        def three(wh, wl, xh, xl, m_w=(None, None), m_x=(None, None)):
            return [(wh, xh, m_w[0], m_x[0]), (wl, xh, m_w[1]), (wh, xl, m_x[1])]

        def first(it, out, wcols, m_w=(None, None)):
            wh, wl = wcols
            i, bk = zb.take()
            pe.wait(zb.freed[i])
            o = bk[:, 0:it.n]
            if it.w != P:
                o = o.rearrange("p (b t) -> p b t", t=it.w)
            xh, xl = xs(it)
            out.append((i, bk, matmuls(o, three(wh, wl, xh, xl, m_w, m_feat[it.blk]))))

        def up(it):
            it.z = []
            if it.kind == "A":
                a = it.f * P
                first(it, it.z, (WAH[:, it.ex, a:a + P], WAL[:, it.ex, a:a + P]),
                      m_wA[it.ex][0])
            elif it.kind == "B":
                for k in range(2):
                    a = k * 512 + it.f * P
                    s = it.ex % 2
                    first(it, it.z, (WBH[:, s, a:a + P], WBL[:, s, a:a + P]),
                          m_wB[it.ex][k])
            elif it.kind == "S":
                for k in range(2):
                    a = it.ex * 768 + k * 256 + it.f * P
                    first(it, it.z, (WCH[:, a:a + P], WCL[:, a:a + P]), m_wC["all"])
            elif it.kind == "R":
                a = 1536 + it.ex * 256
                first(it, it.z, (WCH[:, a:a + P], WCL[:, a:a + P]))
            else:
                i, bk = zb.take()
                pe.wait(m_p[it.blk], zb.freed[i])
                it.z.append((i, bk, matmuls(bk[:, :], [(V1S[:, it.f * P:it.f * P + P], PS[:, it.blk % 2, :])])))
            if it.kind == "F":
                m_ps[it.blk] = pe.last()
            else:
                last_up[it.blk] = pe.last()

        n_read = [0] * 8

        def middle(it, k):
            s, g, n = k % NS, k % NG, it.n
            i, bk, m_z = it.z[0]
            f_hf = free_hf[s]
            if it.kind in ("A", "F"):
                fn = ACT.Gelu_apprx_tanh
                if it.kind == "F":
                    bias = col("b1", it.f)
                elif it.ex == 0:
                    bias = col("sb1", it.f)
                else:
                    bias = col("eb1", 4 * (it.ex - 1) + it.f)
                act.wait(m_z, m_sm, *f_hf)
                it.h = zb.freed[i] = act.do(lambda e: e.activation(Hf[:, s, 0:n], bk[:, 0:n], fn, bias=bias))
                return
            act.wait(m_z, free_sg[g])
            fn = ACT.Gelu if it.kind == "R" else ACT.Silu
            m = zb.freed[i] = act.do(lambda e: e.activation(Sg[:, g, :], bk[:, :], fn))
            if it.kind == "R":
                q = CWB[:, it.ex // 4, (it.ex % 4) * BLK:(it.ex % 4) * BLK + BLK]
                pool.wait(m, m_cw["r", it.blk, it.ex], *f_hf)
                it.h = pool.do(lambda e: e.tensor_tensor(Hf[:, s, :], Sg[:, g, :], q, ALU.mult))
                m_cwread["r", it.ex] = [it.h]
                n_read[it.ex] += 1
            else:
                j, bj, m_u = it.z[1]
                dve.wait(m, m_u, *f_hf)
                it.h = zb.freed[j] = dve.do(lambda e: e.tensor_tensor(Hf[:, s, :], bj[:, :], Sg[:, g, :], ALU.mult))
            free_sg[g] = it.h

        def parts(it, k):
            s, hs, n = k % NS, k % NH, it.n
            on_act = it.kind in ("B", "S") or (it.kind == "A" and k % 2) or (it.kind == "R" and k % 2)
            low = pool if it.kind in "ABS" and k % 4 == 1 or it.kind == "F" and k % 2 else dve
            it.parts = split(act if on_act else dve, low, Hf[:, s, 0:n], HH[:, hs, 0:n], HL[:, hs, 0:n],
                             [it.h], [free_h[hs]])
            free_hf[s] = list(it.parts)

        unit = {}

        def down(it, k):
            hs, n = k % NH, it.n
            if it.kind == "A":
                a = 512 + it.f * P
                key, w, ready = "A", (WAH[:, it.ex, a:a + P], WAL[:, it.ex, a:a + P]), m_wA[it.ex][1]
            elif it.kind == "B":
                a = 1024 + it.f * P
                key, w, ready = "B", (WBH[:, it.ex % 2, a:a + P], WBL[:, it.ex % 2, a:a + P]), m_wB[it.ex][2]
            elif it.kind == "F":
                key, w, ready = "F", None, (None, None)
            else:
                a = it.ex * 768 + 512 + it.f * P if it.kind == "S" else 1536 + it.ex * 256 + P
                key, w, ready = "C", (WCH[:, a:a + P], WCL[:, a:a + P]), (None, None)
            if key == "C":
                key = ("C", it.blk)
            new = key not in unit
            if new:
                r = ab if key == "F" else ob
                unit[key] = (r,) + r.take()
                pe.wait(unit[key][0].freed[unit[key][1]])
            r, i, bk = unit[key]
            if key == "F":
                u = U2S[:, it.f, :, :].rearrange("p r c -> p (r c)")
                pairs = [(u, HH[:, hs, :], it.parts[0]), (u, HL[:, hs, :], it.parts[1])]
            else:
                pairs = three(*w, HH[:, hs, 0:n], HL[:, hs, 0:n], ready, it.parts)
            m = free_h[hs] = matmuls(bk[:, 0:n], pairs, start=new, stop=it.last)
            if it.kind == "A":
                last_down["A"] = m
            if it.kind == "B":
                last_down["B", it.ex] = m
            if it.last:
                del unit[key]
                it.o = (r, i, bk, m)
                return True

        def finish(it):
            r, i, bk, m = it.o
            c = it.blk % 2
            t = k_tmp[0] % 2
            n, w = it.n, it.w
            if it.kind == "A":
                if it.ex == 0:
                    dve.wait(m, m_sm, *(cbf[c] or []))
                    m_acc[c] = r.freed[i] = dve.do(lambda e: e.tensor_scalar(CB[:, c, :], bk[:, :], col("sb2"), None,
                                                                             ALU.add))
                    return
                ex = it.ex - 1
                k_tmp[0] += 1
                assert m_g[0]
                dve.wait(m, m_g[0], m_tmp[t])
                wg = WG[:, 4 * it.blk:4 * it.blk + 4, ex:ex + 1].to_broadcast([P, 4, w])
                v = lambda a: a[:, 0:n].rearrange("p (b t) -> p b t", t=w)
                md = r.freed[i] = dve.do(lambda e: e.scalar_tensor_tensor(
                    out=v(TMP[:, t, :]), in0=v(bk), scalar=col("eb2", ex), in1=wg, op0=ALU.add, op1=ALU.mult))
                acc = CB[:, c, :].rearrange("p (b t) -> p b t", t=P)[:, :, it.lo:it.hi]
                pool.wait(md, m_acc[c])
                m_acc[c] = m_tmp[t] = pool.do(lambda e: e.tensor_tensor(acc, acc, v(TMP[:, t, :]), ALU.add))
                if it.ex == 4:
                    gens.append(close_a(it.blk))
            elif it.kind == "B":
                k_tmp[0] += 1
                g = it.blk // 4
                q = CWB[:, g, (it.blk % 4) * BLK:(it.blk % 4) * BLK + BLK]
                dve.wait(m, m_cw[g, it.ex], m_tmp[t])
                md = r.freed[i] = dve.do(lambda e: e.tensor_tensor(TMP[:, t, :], bk[:, :], q, ALU.mult))
                m_cwread[g] = [md]
                if it.blk % 4 == 3:
                    if it.ex < 7:
                        load_cw(g, it.ex + 1)
                    else:
                        for e in range(4 * g, 4 * g + 4):
                            m_cwread["r", e] = [md]
                xt = XT[:, it.blk, :]
                pool.wait(md, m_xt[it.blk])
                m_tmp[t] = m_xt[it.blk] = pool.do(lambda e: e.tensor_tensor(xt, xt, TMP[:, t, :], ALU.add))
                if it.ex == 7:
                    gens.append(close_b(it.blk))
            elif it.kind == "R":
                gens.append(close_c(it))
            else:
                gens.append(close_f(it))

        def close_a(blk):
            c = blk % 2
            m = m_acc[c]
            yield from pause(2)
            parts_ = split(act, dve, CB[:, c, :], XH[:, blk, :], XL[:, blk, :], [m], [last_up[blk]])
            m_feat[blk] = list(parts_)
            yield from pause(3)
            i, bk = ab.take()
            pe.wait(m, m_sm, ab.freed[i])
            for t in range(4):
                mk = matmuls(bk[:, t * 16:t * 16 + 16], [(CB[:, c, t * P:t * P + P], S("rw"))])
            cbf[c] = [*parts_, mk]
            yield
            dve.wait(mk)
            ab.freed[i] = dve.do(lambda e: e.tensor_copy(LR[:, 4 * blk:4 * blk + 4, :],
                                                         bk[:, 0:64].rearrange("p (t e) -> p t e", e=16)))
            if blk % 4 == 3:
                yield
                yield from route0(blk // 4)

        def close_b(blk):
            yield
            parts_ = split(act, dve, XT[:, blk, :], XH[:, blk, :], XL[:, blk, :], [m_xt[blk]], [last_up[blk]])
            m_feat[blk] = list(parts_)
            yield from pause(1 if blk == 3 else 2)
            i, bk = ab.take()
            pe.wait(m_xt[blk], ab.freed[i])
            for t in range(4):
                mk = matmuls(bk[:, t * 8:t * 8 + 8], [(XT[:, blk, t * P:t * P + P], S("wrx"))])
            yield
            dve.wait(mk)
            ab.freed[i] = dve.do(lambda e: e.tensor_tensor(
                LR[:, 4 * blk:4 * blk + 4, 0:8], bk[:, 0:32].rearrange("p (t e) -> p t e", e=8),
                TP[:, 4 * blk:4 * blk + 4, :], ALU.add))
            if blk % 4 == 3:
                yield from pause(1)
                yield from route1(blk // 4)

        next_gate = [0] * 8

        def load_gates():
            for e, b in enumerate(next_gate):
                if b < NBLK and (1, b // 4) in m_scr and ("r", e) in m_cwread and n_read[e] == b:
                    load_gate(b, e)
                    next_gate[e] += 1

        m_p = {}
        m_ph = [None]
        m_ps = {}
        m_qs = [None]

        def close_c(it):
            r, i, bk, m = it.o
            blk = it.blk
            t = k_tmp[0] % 2
            k_tmp[0] += 1
            act.wait(m, m_tmp[t])
            mt = r.freed[i] = act.do(lambda e: e.activation(TMP[:, t, :], bk[:, :], ACT.Copy, scale=0.25))
            parts_ = split(dve, dve, TMP[:, t, :], XH[:, blk, :], XL[:, blk, :], [mt], [last_up[blk]])
            m_tmp[t] = parts_[1]
            yield from pause(5)
            j, bj = zb.take()
            pe.wait(zb.freed[j])
            m = matmuls(bj[:, :], three(U1H[:, :], U1L[:, :], XH[:, blk, :], XL[:, blk, :], m_wC["all"], parts_))
            last_up[blk] = m
            act.wait(m, m_ph[0])
            mh = act.do(lambda e: e.activation(PH[:, :], bj[:, :], ACT.Copy))
            dve.wait(mh, m, m_ps.get(blk - 2))
            m_p[blk] = zb.freed[j] = dve.do(lambda e: e.scalar_tensor_tensor(
                out=PS[:, blk % 2, :], in0=PH[:, :].bitcast(F32), scalar=col("m1"), in1=bj[:, :], op0=ALU.mult,
                op1=ALU.add))
            m_ph[0] = m_p[blk]

        def close_f(it):
            r, i, bk, m = it.o
            blk = it.blk
            act.wait(m, m_ph[0])
            mh = act.do(lambda e: e.activation(PH[:, :], bk[:, :], ACT.Copy))
            dve.wait(mh, m, m_qs[0])
            mq = r.freed[i] = m_ph[0] = dve.do(lambda e: e.scalar_tensor_tensor(
                out=QS[:, :], in0=PH[:, :].bitcast(F32), scalar=col("m2"), in1=bk[:, :], op0=ALU.mult, op1=ALU.add))
            yield from pause(4)
            j, bj = ab.take()
            pe.wait(mq, ab.freed[j])
            m = matmuls(bj[:, :], [(V2H[:, :], QS[:, :]), (V2L[:, :], QS[:, :])])
            m_qs[0] = m
            yield
            c = blk % 2
            dve.wait(m, *(cbf[c] or []))
            my = ab.freed[j] = dve.do(lambda e: e.scalar_tensor_tensor(
                out=CB[:, c, :], in0=bj[:, :], scalar=col("b2"), in1=XT[:, blk, :], op0=ALU.add, op1=ALU.add))
            sp.wait(my)
            cbf[c] = [fout_b[blk].dma(sp, out_d[:, blk * BLK:blk * BLK + BLK], CB[:, c, :])]
            m_out.append(cbf[c][0])

        fout_b = [flow(f"f_o{i}") for i in range(NBLK)]

        items = plan()
        first_slot = {}
        for k, it in enumerate(items):
            if it is None:
                continue
            first_slot.setdefault((it.kind, it.ex), k)
            first_slot.setdefault(("blk", it.kind, it.blk), k)
        gens = []
        starts = {1: [prep_a()], 2: [gates()], 12: [prep_x()], first_slot["blk", "A", 5]: [prep_b(0)],
                  first_slot["B", 1] + LAG + 12: [prep_c()]}
        for ex in range(1, 8):
            starts.setdefault(first_slot["B", ex - 1] + (LAG - 3 if ex > 1 else LAG + 2 + 8), []).append(prep_b(ex))

        n = len(items)
        for k in range(n + LAG + 20):
            load_gates()
            gens += starts.get(k, [])
            live = []
            for g in gens[:]:
                try:
                    next(g)
                    live.append(g)
                except StopIteration:
                    pass
            gens[:] = live
            for b in range(NBLK):
                if m_feat[b] is None and m_split_x[b]:
                    m_feat[b] = list(m_split_x[b])
            if k < n and items[k]:
                up(items[k])
                middle(items[k], k)
            if 1 <= k <= n and items[k - 1]:
                parts(items[k - 1], k - 1)
            if LAG <= k < n + LAG and items[k - LAG]:
                it = items[k - LAG]
                if down(it, k - LAG):
                    finish(it)
        assert not gens and len(m_out) == NBLK
        sp.wait(*m_out, *m_scr.values())

        block = ctx.enter_context(nc.Block())

        @block.sync
        def _(e):
            sp.run(e)

        @block.tensor
        def _(e):
            pe.run(e)

        @block.scalar
        def _(e):
            act.run(e)

        @block.vector
        def _(e):
            dve.run(e)

        @block.gpsimd
        def _(e):
            pool.run(e)


def kernel(**inputs):
    import numpy as np
    import concourse.bacc as bacc
    from concourse.bass_utils import run_bass_kernel_spmd

    a = {k: np.asarray(v) for k, v in inputs.items()}
    f32 = np.float32
    perm = np.r_[0:42, 84:128, 42:84]

    def rows(w):
        return w.reshape(-1, P, w.shape[-1]).transpose(1, 0, 2).reshape(P, -1)

    def cols(v):
        return v.reshape(-1, P).T

    def every(v):
        return np.broadcast_to(v.reshape(1, -1), (P, v.size))

    x = a["x"][:, perm, :].reshape(NT, P).T
    part = np.arange(P)[:, None] // 32
    wr = a["L1_cond_W_router"]
    small = {
        "gw": rows(a["L0_cond_gate_w"]), "tw": a["L0_cond_time_w"], "wrx": wr[:, :P].T, "wrt": wr[:, P:].T,
        "rw": np.concatenate([a["L0_ffn_w_router"], a["L0_ffn_w_gating"]], 1),
        "gb": every(a["L0_cond_gate_b"]), "tb": every(a["L0_cond_time_b"]), "rb": every(a["L1_cond_router_bias"]),
        "eb1": cols(a["L0_cond_eb1"]), "sb1": cols(a["L0_cond_sb1"]), "eb2": cols(a["L0_cond_eb2"]),
        "sb2": cols(a["L0_cond_sb2"]), "b1": cols(a["L1_ffn_b1"]), "b2": cols(a["L1_ffn_b2"]),
        "cond": a["cond_1024"].T,
        "tri8": every(np.tril(np.ones((8, 8), f32), -1)), "tri4": every(np.tril(np.ones((4, 4), f32), -1)),
        "m1": -(part % 2).astype(f32), "m2": -(part // 2).astype(f32),
        "ident": np.eye(P, dtype=f32), "ones": np.ones((P, P), f32),
    }
    small = np.concatenate([small[n] for n in SM], 1)
    wa = [a["L0_cond_sw1"], rows(a["L0_cond_sw2"])]
    for e in range(4):
        wa += [a["L0_cond_ew1"][e], rows(a["L0_cond_ew2"][e])]
    wb = np.stack([np.concatenate([a["L0_ffn_w_gate"][e], a["L0_ffn_w_up"][e], rows(a["L0_ffn_w_down"][e])], 1)
                   for e in range(8)])
    wc = []
    for e in range(2):
        wc += [a["L1_cond_s_w1"][e].T, a["L1_cond_s_w3"][e].T, rows(a["L1_cond_s_w2"][e].T)]
    for e in range(8):
        wc += [a["L1_cond_r_w1"][e].T, a["L1_cond_r_w2"][e].T]
    u2 = rows(np.tile(a["L1_ffn_U2"], (1, 4)))
    wf = [np.tile(a["L1_ffn_U1"], (1, 4)), np.tile(a["L1_ffn_V1"], (4, 1)), u2, np.tile(a["L1_ffn_V2"], (4, 1))]

    nc = bacc.Bacc("TRN2", target_bir_lowering=False, num_devices=1)
    arrays, args = {}, []
    for name, v in [("x", x), ("small", small), ("wa", np.concatenate(wa, 1)), ("wb", wb),
                    ("wc", np.concatenate(wc, 1)), ("wf", np.concatenate(wf, 1))]:
        v = np.ascontiguousarray(v)
        arrays[f"in_{name}_dram"] = v
        args.append(nc.dram_tensor(f"in_{name}_dram", v.shape, mybir.dt.from_np(v.dtype), kind="ExternalInput").ap())
    args.append(nc.dram_tensor("scratch", (2, 2, P, P), F32, kind="Internal").ap())
    args.append(nc.dram_tensor("out_0_dram", (P, NT), F32, kind="ExternalOutput").ap())
    build(nc, *args)
    r = run_bass_kernel_spmd(nc, [arrays], core_ids=[0])
    y = r.results[0]["out_0_dram"].T.reshape(NB, P, P)
    back = np.argsort(perm)
    return np.ascontiguousarray(y[:, back, :])
```
